# Optimizing a Trainium2 kernel written in Bass

```python
import numpy as np
import jax
import jax.numpy as jnp

def _softmax(x, axis=-1):
    return jax.nn.softmax(x, axis=axis)

def _gelu(x):
    return jax.nn.gelu(x, approximate=True)

def _silu(x):
    return jax.nn.silu(x)

def _sigmoid(x):
    return jax.nn.sigmoid(x)

def _layernorm(x, axis=-1, eps=1e-05):
    m = jnp.mean(x, axis=axis, keepdims=True)
    v = jnp.var(x, axis=axis, keepdims=True)
    return (x - m) / jnp.sqrt(v + eps)

def _scatter_add(tgt, idx, src, axis=0):
    return tgt.at[idx].add(src)

def _segment_sum(src, seg, n):
    return jax.ops.segment_sum(src, seg, n)
kernel_name = 'mk_hybrid_d1_jaxref_r8_93f192'

def setup_inputs(seed: int=0):
    np.random.seed(seed)
    _w = jnp.asarray

    def _L0_attn_a_setup():
        import jax, jax.numpy as jnp
        import numpy as np
        D_MODEL = 128
        NUM_HEADS = 16
        HEAD_DIM = D_MODEL // NUM_HEADS
        BATCH = 4
        SEQ = 256

        def circulant(x, c, b):
            d = c.shape[0]
            y = jnp.fft.irfft(jnp.fft.rfft(x, axis=-1) * jnp.fft.rfft(c), n=d, axis=-1)
            return y + b
        key = jax.random.key(seed)
        ks = jax.random.split(key, 9)
        scale = 1.0 / np.sqrt(D_MODEL)
        inp = {'x': jax.random.normal(ks[0], (BATCH, SEQ, D_MODEL), dtype=jnp.float32), 'wq_c': jax.random.normal(ks[1], (D_MODEL,), dtype=jnp.float32) * scale, 'wq_b': jnp.zeros((D_MODEL,), dtype=jnp.float32), 'wk_c': jax.random.normal(ks[2], (D_MODEL,), dtype=jnp.float32) * scale, 'wk_b': jnp.zeros((D_MODEL,), dtype=jnp.float32), 'wv_c': jax.random.normal(ks[3], (D_MODEL,), dtype=jnp.float32) * scale, 'wv_b': jnp.zeros((D_MODEL,), dtype=jnp.float32), 'wo_c': jax.random.normal(ks[4], (D_MODEL,), dtype=jnp.float32) * scale, 'wo_b': jnp.zeros((D_MODEL,), dtype=jnp.float32)}
        return inp
    _L0_attn_a_in = _L0_attn_a_setup()

    def _L0_attn_b_setup():
        import jax, jax.numpy as jnp
        import numpy as np
        import math
        B, S, D, H, R, DFF = (4, 128, 128, 16, 64, 512)

        def _layernorm(x, g, b, eps=1e-05):
            m = jnp.mean(x, axis=-1, keepdims=True)
            v = jnp.var(x, axis=-1, keepdims=True)
            return (x - m) / jnp.sqrt(v + eps) * g + b
        key = jax.random.key(seed)
        ks = jax.random.split(key, 12)
        sc = 0.02
        return {'src': jax.random.normal(ks[0], (B, S, D), jnp.float32), 'in_proj_w': jax.random.normal(ks[1], (3 * D, D), jnp.float32) * sc, 'in_proj_b': jnp.zeros((3 * D,), jnp.float32), 'out_proj_w': jax.random.normal(ks[2], (D, D), jnp.float32) * sc, 'out_proj_b': jnp.zeros((D,), jnp.float32), 'Qp_w': jax.random.normal(ks[3], (R, D), jnp.float32) * sc, 'Qp_b': jnp.zeros((R,), jnp.float32), 'Kp_w': jax.random.normal(ks[4], (R, D), jnp.float32) * sc, 'Kp_b': jnp.zeros((R,), jnp.float32), 'Vp_w': jax.random.normal(ks[5], (D, D), jnp.float32) * sc, 'Vp_b': jnp.zeros((D,), jnp.float32), 'lam': jnp.float32(0.5), 'ff1_w': jax.random.normal(ks[6], (DFF, D), jnp.float32) * sc, 'ff1_b': jnp.zeros((DFF,), jnp.float32), 'ff2_w': jax.random.normal(ks[7], (D, DFF), jnp.float32) * sc, 'ff2_b': jnp.zeros((D,), jnp.float32), 'ln1_g': jnp.ones((D,), jnp.float32), 'ln1_b': jnp.zeros((D,), jnp.float32), 'ln2_g': jnp.ones((D,), jnp.float32), 'ln2_b': jnp.zeros((D,), jnp.float32)}
    _L0_attn_b_in = _L0_attn_b_setup()

    def _L0_ffn_setup():
        import jax, jax.numpy as jnp
        import numpy as np
        CAPACITY_FACTOR = 0.5
        key = jax.random.key(seed)
        ks = jax.random.split(key, 5)
        B, S, D, F = (4, 512, 128, 512)
        scale_in = 1.0 / np.sqrt(D)
        scale_ff = 1.0 / np.sqrt(F)
        return {'hidden_states': jax.random.normal(ks[0], (B, S, D), dtype=jnp.float32), 'w_router': jax.random.normal(ks[1], (D,), dtype=jnp.float32) * scale_in, 'W1': jax.random.normal(ks[2], (D, F), dtype=jnp.float32) * scale_in, 'b1': jnp.zeros((F,), dtype=jnp.float32), 'W2': jax.random.normal(ks[3], (F, D), dtype=jnp.float32) * scale_ff, 'b2': jnp.zeros((D,), dtype=jnp.float32)}
    _L0_ffn_in = _L0_ffn_setup()
    _d = {'L0_attn_a_x': _L0_attn_a_in['x'], 'L0_attn_a_wq_c': _L0_attn_a_in['wq_c'], 'L0_attn_a_wq_b': _L0_attn_a_in['wq_b'], 'L0_attn_a_wk_c': _L0_attn_a_in['wk_c'], 'L0_attn_a_wk_b': _L0_attn_a_in['wk_b'], 'L0_attn_a_wv_c': _L0_attn_a_in['wv_c'], 'L0_attn_a_wv_b': _L0_attn_a_in['wv_b'], 'L0_attn_a_wo_c': _L0_attn_a_in['wo_c'], 'L0_attn_a_wo_b': _L0_attn_a_in['wo_b'], 'L0_attn_b_in_proj_w': _L0_attn_b_in['in_proj_w'], 'L0_attn_b_in_proj_b': _L0_attn_b_in['in_proj_b'], 'L0_attn_b_out_proj_w': _L0_attn_b_in['out_proj_w'], 'L0_attn_b_out_proj_b': _L0_attn_b_in['out_proj_b'], 'L0_attn_b_Qp_w': _L0_attn_b_in['Qp_w'], 'L0_attn_b_Qp_b': _L0_attn_b_in['Qp_b'], 'L0_attn_b_Kp_w': _L0_attn_b_in['Kp_w'], 'L0_attn_b_Kp_b': _L0_attn_b_in['Kp_b'], 'L0_attn_b_Vp_w': _L0_attn_b_in['Vp_w'], 'L0_attn_b_Vp_b': _L0_attn_b_in['Vp_b'], 'L0_attn_b_lam': _L0_attn_b_in['lam'], 'L0_attn_b_ff1_w': _L0_attn_b_in['ff1_w'], 'L0_attn_b_ff1_b': _L0_attn_b_in['ff1_b'], 'L0_attn_b_ff2_w': _L0_attn_b_in['ff2_w'], 'L0_attn_b_ff2_b': _L0_attn_b_in['ff2_b'], 'L0_attn_b_ln1_g': _L0_attn_b_in['ln1_g'], 'L0_attn_b_ln1_b': _L0_attn_b_in['ln1_b'], 'L0_attn_b_ln2_g': _L0_attn_b_in['ln2_g'], 'L0_attn_b_ln2_b': _L0_attn_b_in['ln2_b'], 'L0_ffn_w_router': _L0_ffn_in['w_router'], 'L0_ffn_W1': _L0_ffn_in['W1'], 'L0_ffn_b1': _L0_ffn_in['b1'], 'L0_ffn_W2': _L0_ffn_in['W2'], 'L0_ffn_b2': _L0_ffn_in['b2']}
    _x0 = _d['L0_attn_a_x']
    _d['L0_attn_a_x'] = jax.random.normal(jax.random.fold_in(jax.random.key(seed), 1), (4, 512, 128), dtype=_x0.dtype)
    del _x0
    return _d

def reference(L0_attn_a_x, L0_attn_a_wq_c, L0_attn_a_wq_b, L0_attn_a_wk_c, L0_attn_a_wk_b, L0_attn_a_wv_c, L0_attn_a_wv_b, L0_attn_a_wo_c, L0_attn_a_wo_b, L0_attn_b_in_proj_w, L0_attn_b_in_proj_b, L0_attn_b_out_proj_w, L0_attn_b_out_proj_b, L0_attn_b_Qp_w, L0_attn_b_Qp_b, L0_attn_b_Kp_w, L0_attn_b_Kp_b, L0_attn_b_Vp_w, L0_attn_b_Vp_b, L0_attn_b_lam, L0_attn_b_ff1_w, L0_attn_b_ff1_b, L0_attn_b_ff2_w, L0_attn_b_ff2_b, L0_attn_b_ln1_g, L0_attn_b_ln1_b, L0_attn_b_ln2_g, L0_attn_b_ln2_b, L0_ffn_w_router, L0_ffn_W1, L0_ffn_b1, L0_ffn_W2, L0_ffn_b2):

    def _L0_attn_a_ref(x, wq_c, wq_b, wk_c, wk_b, wv_c, wv_b, wo_c, wo_b):
        import jax, jax.numpy as jnp
        import numpy as np
        D_MODEL = 128
        NUM_HEADS = 16
        HEAD_DIM = D_MODEL // NUM_HEADS
        BATCH = 4
        SEQ = 256

        def circulant(x, c, b):
            d = c.shape[0]
            y = jnp.fft.irfft(jnp.fft.rfft(x, axis=-1) * jnp.fft.rfft(c), n=d, axis=-1)
            return y + b
        bs, seq_len, dm = x.shape
        Q = circulant(x, wq_c, wq_b)
        K = circulant(x, wk_c, wk_b)
        V = circulant(x, wv_c, wv_b)
        Q = Q.reshape(bs, seq_len, NUM_HEADS, HEAD_DIM)
        K = K.reshape(bs, seq_len, NUM_HEADS, HEAD_DIM)
        V = V.reshape(bs, seq_len, NUM_HEADS, HEAD_DIM)
        scale = HEAD_DIM ** (-0.5)
        attn_logits = jnp.einsum('bqhd,bkhd->bhqk', Q, K) * scale
        attn_weights = jax.nn.softmax(attn_logits, axis=-1)
        out_heads = jnp.einsum('bhqk,bkhd->bqhd', attn_weights, V)
        out_merge = out_heads.reshape(bs, seq_len, dm)
        out = circulant(out_merge, wo_c, wo_b)
        return out

    def _L0_attn_b_ref(src, in_proj_w, in_proj_b, out_proj_w, out_proj_b, Qp_w, Qp_b, Kp_w, Kp_b, Vp_w, Vp_b, lam, ff1_w, ff1_b, ff2_w, ff2_b, ln1_g, ln1_b, ln2_g, ln2_b):
        import jax, jax.numpy as jnp
        import numpy as np
        import math
        B, S, D, H, R, DFF = (4, 128, 128, 16, 64, 512)

        def _layernorm(x, g, b, eps=1e-05):
            m = jnp.mean(x, axis=-1, keepdims=True)
            v = jnp.var(x, axis=-1, keepdims=True)
            return (x - m) / jnp.sqrt(v + eps) * g + b
        b, s, d = src.shape
        dh = d // H
        qkv = src @ in_proj_w.T + in_proj_b
        q, k, v = jnp.split(qkv, 3, axis=-1)
        q = q.reshape(b, s, H, dh).transpose(0, 2, 1, 3)
        k = k.reshape(b, s, H, dh).transpose(0, 2, 1, 3)
        v = v.reshape(b, s, H, dh).transpose(0, 2, 1, 3)
        scores = jnp.einsum('bhqd,bhkd->bhqk', q, k) / math.sqrt(dh)
        attn = jax.nn.softmax(scores, axis=-1)
        ctx = jnp.einsum('bhqk,bhkd->bhqd', attn, v)
        ctx = ctx.transpose(0, 2, 1, 3).reshape(b, s, d)
        dense_output = ctx @ out_proj_w.T + out_proj_b
        Q = src @ Qp_w.T + Qp_b
        K = src @ Kp_w.T + Kp_b
        V = src @ Vp_w.T + Vp_b
        QK = jnp.einsum('bqr,bkr->bqk', Q, K) / math.sqrt(R)
        aw = jax.nn.softmax(QK, axis=-1)
        kk = max(1, int(s * 0.2))
        topv, topi = jax.lax.top_k(aw, kk)
        bi = jnp.arange(b)[:, None, None]
        si = jnp.arange(s)[None, :, None]
        sparse_attn = jnp.zeros_like(aw).at[bi, si, topi].set(topv)
        sparse_attn = sparse_attn / (jnp.sum(sparse_attn, axis=-1, keepdims=True) + 1e-09)
        sparse_output = jnp.einsum('bqk,bkd->bqd', sparse_attn, V)
        sig = jax.nn.sigmoid(lam)
        fused = sig * dense_output + (1.0 - sig) * sparse_output
        x = _layernorm(src + fused, ln1_g, ln1_b)
        ff = jax.nn.relu(x @ ff1_w.T + ff1_b) @ ff2_w.T + ff2_b
        return _layernorm(x + ff, ln2_g, ln2_b)

    def _L0_ffn_ref(hidden_states, w_router, W1, b1, W2, b2):
        import jax, jax.numpy as jnp
        import numpy as np
        CAPACITY_FACTOR = 0.5
        'Mixture-of-Depths block: route top-k tokens through an FFN inner block,\n            scatter back with sigmoid router weights; bypassed tokens pass through.'
        B, S, D = hidden_states.shape
        k = int(S * CAPACITY_FACTOR)
        scores = jnp.einsum('bsd,d->bs', hidden_states, w_router)
        top_scores, top_idx = jax.lax.top_k(scores, k)
        weights = jax.nn.sigmoid(top_scores)
        selected = jnp.take_along_axis(hidden_states, top_idx[:, :, None], axis=1)
        h = jax.nn.gelu(jnp.einsum('bkd,df->bkf', selected, W1) + b1)
        processed = jnp.einsum('bkf,fd->bkd', h, W2) + b2
        update = weights[:, :, None] * processed

        def scatter_one(xb, ib, ub):
            return xb.at[ib].add(ub)
        output = jax.vmap(scatter_one)(hidden_states, top_idx, update)
        return output
    x = L0_attn_a_x
    x = x + _L0_attn_a_ref(_layernorm(x, axis=-1), L0_attn_a_wq_c, L0_attn_a_wq_b, L0_attn_a_wk_c, L0_attn_a_wk_b, L0_attn_a_wv_c, L0_attn_a_wv_b, L0_attn_a_wo_c, L0_attn_a_wo_b)
    x = x + _L0_ffn_ref(_layernorm(x, axis=-1), L0_ffn_w_router, L0_ffn_W1, L0_ffn_b1, L0_ffn_W2, L0_ffn_b2)
    x = x + _L0_attn_b_ref(_layernorm(x, axis=-1), L0_attn_b_in_proj_w, L0_attn_b_in_proj_b, L0_attn_b_out_proj_w, L0_attn_b_out_proj_b, L0_attn_b_Qp_w, L0_attn_b_Qp_b, L0_attn_b_Kp_w, L0_attn_b_Kp_b, L0_attn_b_Vp_w, L0_attn_b_Vp_b, L0_attn_b_lam, L0_attn_b_ff1_w, L0_attn_b_ff1_b, L0_attn_b_ff2_w, L0_attn_b_ff2_b, L0_attn_b_ln1_g, L0_attn_b_ln1_b, L0_attn_b_ln2_g, L0_attn_b_ln2_b)
    x = x + _L0_ffn_ref(_layernorm(x, axis=-1), L0_ffn_w_router, L0_ffn_W1, L0_ffn_b1, L0_ffn_W2, L0_ffn_b2)
    return x

_drawn_inputs = setup_inputs


def setup_inputs(seed=0):
    import zlib

    import numpy as np

    out = dict(_drawn_inputs(seed))
    spreads = {'L0_attn_a_wq_b': (0.0, 0.678),
     'L0_attn_a_wk_b': (0.0, 0.8),
     'L0_attn_a_wv_b': (0.0, 0.1),
     'L0_attn_a_wo_b': (0.0, 0.1),
     'L0_attn_b_in_proj_b': (0.0, 0.8),
     'L0_attn_b_out_proj_b': (0.0, 0.383),
     'L0_attn_b_Qp_b': (0.0, 0.8),
     'L0_attn_b_Kp_b': (0.0, 0.8),
     'L0_attn_b_Vp_b': (0.0, 0.628),
     'L0_attn_b_ff1_b': (0.0, 0.726),
     'L0_attn_b_ff2_b': (0.0, 0.1),
     'L0_attn_b_ln1_g': (1.0, 0.2),
     'L0_attn_b_ln1_b': (0.0, 0.1),
     'L0_attn_b_ln2_g': (1.0, 0.2),
     'L0_attn_b_ln2_b': (0.0, 0.1),
     'L0_ffn_b1': (0.0, 0.362),
     'L0_ffn_b2': (0.0, 0.1)}
    factors = {'L0_attn_b_in_proj_w': 8.0,
     'L0_attn_b_out_proj_w': 8.0,
     'L0_attn_b_Qp_w': 8.0,
     'L0_attn_b_Kp_w': 8.0,
     'L0_attn_b_Vp_w': 8.0,
     'L0_attn_b_ff1_w': 2.677}
    for name, (base, spread) in spreads.items():
        noise = np.random.default_rng([zlib.crc32(name.encode()), seed]).standard_normal(out[name].shape)
        drawn = base * np.exp(spread * noise) if base else spread * noise
        out[name] = jnp.asarray(drawn.astype(out[name].dtype))
    for name, factor in factors.items():
        out[name] = (out[name] * factor).astype(out[name].dtype)
    return out
```

```python
from contextlib import ExitStack

import numpy as np
import concourse.bass as bass
import concourse.mybir as mybir
from concourse.alu_op_type import AluOpType as ALU

ACT = mybir.ActivationFunctionType
AX = mybir.AxisListType
F32 = mybir.dt.float32
BF16 = mybir.dt.bfloat16
ds = bass.ds

P = 128
B, SEQ, D = 4, 512, 128
T = SEQ // P
H, DH = 16, 8
G = 4
HG = H // G
PARTS = 3
SLOT = PARTS * DH
MROW = 96
VW = 32
FF = 512
FT = FF // P
R = 64
KEEP = int(SEQ * 0.2)
ROUTED = SEQ // 2
LAG = 6
EPS = 1e-5
SCALE = DH ** -0.5
DMA = 16
STACK_DMAS = 7


def build(nc, t):
    with ExitStack() as ctx:
        def sb(name, shape, dt=F32):
            return ctx.enter_context(nc.sbuf_tensor(name, shape, dt))

        def ps(name, shape, dt=F32):
            return ctx.enter_context(nc.psum_tensor(name, shape, dt))

        sems = {}

        def sem(name):
            if name not in sems:
                sems[name] = ctx.enter_context(nc.semaphore(name))
            return sems[name]

        ident = sb("ident", [P, P])
        earlier = sb("earlier", [P, T, SEQ], BF16)
        w = {k: sb(f"w_{k}", [P, 3, P]) for k in "AB"}
        wo = {k: sb(f"wo_{k}", [P, P]) for k in "AB"}
        wr_col = sb("wr_col", [P, 1])
        wr = sb("wr", [P, P])
        w1 = sb("w1", [P, FF])
        w2 = sb("w2", [P, FT, D])
        ff1 = sb("ff1", [P, FF])
        ff2 = sb("ff2", [P, FT, D])
        wqp = sb("wqp", [P, 2, P])
        wvp = sb("wvp", [P, P])
        colb = {k: sb(f"colb_{k}", [P, 2]) for k in "AB"}
        colp = sb("colp", [P, 2])
        col1 = {"F": sb("col_b1", [P, FT]), "L": sb("col_ff1b", [P, FT])}
        rows = {}
        for name in ("bv_A", "bo_A", "bv_B", "bo_B", "bvp", "b2", "ff2b", "g1", "be1", "g2", "be2"):
            rows[name] = sb(f"row_{name}", [P, P])
        lam = sb("lam", [P, 1])
        sig = sb("sig", [P, 4])
        half = sb("half", [P, T])
        eps = sb("eps", [P, T])
        idle = sb("idle", [1, 1])

        x = sb("x", [P, B * T, D])
        LNS = ("A", "F1", "B", "L1", "L2", "F2")
        stats = {k: sb(f"stats_{k}", [P, T, 6]) for k in LNS}
        mv = {k: sb(f"mv_{k}", [P, T, 2]) for k in LNS}
        vare = {k: sb(f"vare_{k}", [P, T]) for k in LNS}
        rstd = {k: sb(f"rstd_{k}", [P, T]) for k in LNS}
        xn = {k: sb(f"xn_{k}", [P, T, D]) for k in LNS}
        xnT = {"A": sb("xnT_att", [P, SEQ]), "F1": sb("xnT_ffn", [P, SEQ])}
        xnT.update(B=xnT["A"], L1=xnT["F1"], F2=xnT["F1"])

        qf = sb("qf", [P, 2, SEQ])
        qr = sb("qr", [P, SEQ])
        split = sb("split", [P, 2, PARTS, SEQ], BF16)
        qst = sb("qst", [P, H, SEQ], BF16)
        kst = sb("kst", [P, H, SEQ], BF16)
        zrows = sb("zrows", [PARTS, SEQ], BF16)
        vstage = sb("vstage", [P, T, D])
        vp = sb("vp", [P, T, H, VW])
        negm = sb("negm", [P, G, HG * T])
        mres = sb("mres", [HG * T, P])
        msp = sb("msp", [HG * T, PARTS, P], BF16)
        pT = [sb(f"pT{n}", [P, HG, 2, SEQ]) for n in range(2)]
        oT = sb("oT", [P, SEQ])
        rden = sb("rden", [P, T, HG, 1])
        ctxt = sb("ctxt", [P, T, D])
        ctxT = sb("ctxT", [P, SEQ])
        proj = sb("proj", [P, T, D])

        srow = sb("srow", [P, SEQ])
        junk = sb("junk", [P, T, SEQ], BF16)
        scol = sb("scol", [P, T])
        rank = sb("rank", [P, 2, T])
        gate = sb("gate", [P, 5, T])
        hT = sb("hT", [P, FT, SEQ])
        upd = sb("upd", [P, T, D])

        qkT = sb("qkT", [P, 2, SEQ])
        vsp = sb("vsp", [P, T, D])
        smax = sb("smax", [P, 2, T])
        E = sb("E", [P, T, SEQ])
        W = sb("W", [P, T, SEQ])
        top = sb("top", [P, T, 8])
        sall = sb("sall", [P, T])
        ssel = sb("ssel", [P, T])
        rsp = sb("rsp", [P, 2, T])
        ET = E[:, :, :].rearrange("p t (k q) -> p t k q", q=P)
        so = sb("so", [P, T, D])
        x1 = sb("x1", [P, T, D])
        x1n = sb("x1n", [P, T, D])
        y1 = sb("y1", [P, T, D])

        sbank = [ps(f"sbank{n}", [P, SEQ]) for n in range(2)]
        stb = [ps(f"stb{n}", [P, 2, SEQ]) for n in range(2)]
        pv = ps("pv", [P, SEQ])
        misc = ps("misc", [P, SEQ])
        misc_t = misc[:, :].rearrange("p (t d) -> p t d", t=T)

        qd = nc.dram_tensor("q_parts", (H, PARTS, DH, SEQ), BF16, kind="Internal").ap()
        kd = nc.dram_tensor("k_parts", (H, 2 * PARTS - 1, DH, SEQ), BF16, kind="Internal").ap()
        x_tiles = t["x"].rearrange("(t p) d -> p t d", p=P)
        o_tiles = t["out"].rearrange("(t p) d -> p t d", p=P)

        class Steps:

            def __init__(self, eng, name, b, n):
                self.eng, self.sem, self.base, self.n, self.k = eng, sem(name), b * n, n, 0

            def did(self, ins):
                ins.then_inc(self.sem, 1)
                self.k += 1

            def wait(self):
                self.eng.wait_ge(self.sem, self.base + self.k)

            def end(self):
                assert self.k == self.n, (self.k, self.n)

        def apart(dve):
            dve.memset(idle[:, :], 0.0)

        block = ctx.enter_context(nc.Block())

        X_READY = {"A": ("x_in", DMA), "F1": ("x_attn", 1), "B": ("x_ffn1", 1), "L1": ("x1_ready", 1),
                   "L2": ("y1_ready", 1), "F2": ("x_layer", 1)}
        X_DONE = {"F1": "x_ffn1", "F2": "x_ffn2"}

        def source(k, b, i):
            if k == "L1":
                return x1[:, i, :]
            if k == "L2":
                return y1[:, i, :]
            return x[:, ds(b * T + i, 1), :]

        def bc(row):
            return rows[row][:, :].unsqueeze(1).broadcast_to([P, T, D])

        @block.sync
        def _(sp):
            def load(dst, src, name):
                sp.dma_start(dst, src).then_inc(sem(name), DMA)

            with sp.Fori(0, B) as b:
                load(x[:, ds(b * T, T), :], x_tiles[:, ds(b * T, T), :], "x_in")
            for k in "AB":
                load(w[k][:, :, :], t[f"w_{k}"], "w_in")
                load(wo[k][:, :], t[f"wo_{k}"], "w_in")
                for j in range(2):
                    load(colb[k][:, j:j + 1], t[f"b_{k}"][j * D:(j + 1) * D].unsqueeze(1), "w_in")
                load(rows[f"bv_{k}"][:, :], t[f"b_{k}"][2 * D:3 * D].partition_broadcast(P), "w_in")
                load(rows[f"bo_{k}"][:, :], t[f"bo_{k}"].partition_broadcast(P), "w_in")
            load(wr_col[:, :], t["wr"].unsqueeze(1), "w_in")
            load(w1[:, :], t["W1"], "w_in")
            load(w2[:, :, :], t["W2"].rearrange("(f p) d -> p f d", p=P), "w_in")
            load(ff1[:, :], t["ff1T"], "w_in")
            load(ff2[:, :, :], t["ff2T"].rearrange("(f p) d -> p f d", p=P), "w_in")
            sp.wait_ge(sem("zeros"), 2)
            for j, k in enumerate("QK"):
                load(wqp[:, j, 0:R], t[f"{k}pT"], "w_in")
                load(colp[0:R, j:j + 1], t[f"{k}pb"].unsqueeze(1), "w_in")
            load(wvp[:, :], t["VpT"], "w_in")
            load(col1["F"][:, :], t["b1"], "w_in")
            load(col1["L"][:, :], t["ff1b"], "w_in")
            for row, name in (("bvp", "Vpb"), ("b2", "b2"), ("ff2b", "ff2b"), ("g1", "ln1g"), ("be1", "ln1b"),
                              ("g2", "ln2g"), ("be2", "ln2b")):
                load(rows[row][:, :], t[name].partition_broadcast(P), "w_in")
            load(lam[:, :], t["lam"].partition_broadcast(P), "w_in")

            def store_parts(r):
                sp.wait_ge(sem("parts"), at["split"])
                for g in range(G):
                    sp.wait_ge(sem(f"stack_in{g}"), at["restacked"])
                for s in range(PARTS):
                    sp.dma_start(qd[:, s, :, :], split[:, 0, s, :]).then_inc(sem("parts_out"), DMA)
                for s in range(2 * PARTS - 1):
                    sp.dma_start(kd[:, s, :, :], split[:, 1, s % PARTS, :]).then_inc(sem("parts_out"), DMA)
                sp.wait_ge(sem("parts_out"), at["stored"])

            def fill_stacks(r, g):
                heads = slice(g * HG, (g + 1) * HG)
                sp.wait_ge(sem("st_done"), at["st_over"])
                done = sem(f"stack_in{g}")
                for n, first in enumerate((0, 2, 1)):
                    lines = slice(n * SLOT, (n + 1) * SLOT)
                    sp.dma_start(qst[lines, heads, :], qd[heads, :, :, :].rearrange("h s d t -> (s d) h t")
                                 ).then_inc(done, DMA)
                    sp.dma_start(kst[lines, heads, :],
                                 kd[heads, first:first + PARTS, :, :].rearrange("h s d t -> (s d) h t")
                                 ).then_inc(done, DMA)
                sp.dma_start(qst[MROW:MROW + PARTS, heads, :],
                             zrows[:, :].unsqueeze(1).broadcast_to([PARTS, HG, SEQ])).then_inc(done, DMA)

            def fill_max(r, g):
                sp.wait_ge(sem("max_parts"), at[g])
                for s in range(PARTS):
                    sp.dma_start(qst[MROW + s:MROW + s + 1, g * HG:(g + 1) * HG, :], msp[:, s, :]
                                 ).then_inc(sem(f"mrow_in{g}"), DMA)

            sp.wait_ge(sem("stack_init"), 4)
            at = {}

            def rounds(r):
                values = {"split": 2 * r + 2, "restacked": STACK_DMAS * r * DMA,
                          "stored": DMA * (3 * PARTS - 1) * (r + 1), "st_over": r * H * 2}
                values.update({g: G * r + g + 1 for g in range(G)})
                at.update({k: sp.snap(v) for k, v in values.items()})
                store_parts(r)
                for g in range(G):
                    fill_stacks(r, g)
                for g in range(G):
                    fill_max(r, g)

            with sp.Fori(0, B) as b:
                rounds(b)
            with sp.Fori(0, B) as b:
                rounds(b + B)
                sp.wait_ge(sem("x_ffn2"), sp.snap(b + 1))
                sp.dma_start(o_tiles[:, ds(b * T, T), :], x[:, ds(b * T, T), :]).then_inc(sem("out"), DMA)
            sp.wait_ge(sem("out"), DMA * B)

        W_DMAS = 2 * 6 + 5 + 4 + 3 + 7 + 1

        @block.gpsimd
        def _(pool):
            pool.memset(wqp[:, :, :], 0.0).then_inc(sem("zeros"), 1)
            pool.memset(colp[:, :], 0.0).then_inc(sem("zeros"), 1)
            pool.memset(half[:, :], -0.5).then_inc(sem("pool_init"), 1)
            pool.memset(eps[:, :], EPS).then_inc(sem("pool_init"), 1)
            pool.memset(ident[:, :], 0.0).then_inc(sem("pool_init"), 1)
            pool.memset(earlier[:, :, :], 1.0).then_inc(sem("pool_init"), 1)
            pool.wait_ge(sem("pool_init"), 4)
            pool.affine_select(out=ident[:, :], in_=ident[:, :], compare_op=ALU.not_equal, fill=1.0, base=0,
                               pattern=[[-1, P]], channel_multiplier=1).then_inc(sem("ident_ready"), 1)
            pool.affine_select(out=earlier[:, :, :], in_=earlier[:, :, :], compare_op=ALU.is_gt, fill=0.0, base=0,
                               pattern=[[P, T], [-1, SEQ]], channel_multiplier=1).then_inc(sem("earlier_ready"), 1)

            def rstds(k, b):
                pool.wait_ge(sem(f"aggr_{k}"), T * (b + 1))
                pool.tensor_tensor(vare[k][:, :], mv[k][:, :, 1], eps[:, :], ALU.add).then_inc(sem(f"vare_{k}"), 1)
                pool.wait_ge(sem(f"vare_{k}"), b + 1)
                pool.tensor_tensor(rstd[k][:, :], vare[k][:, :], half[:, :], ALU.pow).then_inc(sem(f"rstd_{k}"), 1)

            def parts(r, j):
                steps = Steps(pool, "split_steps", 2 * r + j, 2)
                pool.wait_ge(sem("parts"), 2 * r + j)
                pool.wait_ge(sem("proj_done"), 2 * (2 * r + j) + 2)
                pool.wait_ge(sem("parts_out"), DMA * (3 * PARTS - 1) * r)
                steps.did(pool.tensor_tensor(qr[:, :], qf[:, j, :], split[:, j, 0, :], ALU.subtract))
                steps.did(pool.tensor_tensor(split[:, j, 1, :], qf[:, j, :], split[:, j, 0, :], ALU.subtract))
                steps.wait()
                steps.end()
                pool.tensor_tensor(split[:, j, 2, :], qr[:, :], split[:, j, 1, :], ALU.subtract
                                   ).then_inc(sem("parts"), 1)

            def place_v(k, r):
                pool.wait_ge(sem("v_staged"), r + 1)
                pool.wait_ge(sem("pv_done"), G * r)
                pool.tensor_tensor(vp[:, :, :, 0:DH], vstage[:, :, :].rearrange("p t (h d) -> p t h d", h=H),
                                   bc(f"bv_{k}").rearrange("p t (h d) -> p t h d", h=H), ALU.add).then_inc(sem("v_ready"), 1)

            pool.wait_ge(sem("stack_init"), 4)
            with pool.Fori(0, B) as b:
                rstds("A", b)
                parts(b, 0)
                parts(b, 1)
                place_v("A", b)
                rstds("F1", b)
            with pool.Fori(0, B) as b:
                rstds("B", b)
                parts(b + B, 0)
                parts(b + B, 1)
                place_v("B", b + B)
                rstds("L1", b)
                rstds("L2", b)
                rstds("F2", b)

        @block.tensor
        def _(pe):
            bank = {}

            def take(freed, count):
                pe.wait_ge(sem(bank["freed"]), bank["count"])
                bank.update(freed=freed, count=count)

            def turn(src, ready, count, signal, freed, freed_count):
                pe.wait_ge(sem(ready), count)
                take(freed, freed_count)
                for i in range(T):
                    last = pe.transpose(misc[:, i * P:(i + 1) * P], src[:, i, :], ident[:, :])
                last.then_inc(sem(signal), 1)

            def token_product(lhsT, rhs, signal, freed, count):
                take(freed, count)
                for i in range(T):
                    last = pe.matmul(misc[:, i * P:(i + 1) * P], lhsT[:, i * P:(i + 1) * P], rhs,
                                     start=True, stop=True)
                last.then_inc(sem(signal), 1)

            def norm_turn(k, b):
                turn(xn[k], f"xn_{k}", b + 1, f"T_{k}", f"xnT_{k}", b + 1)
                pe.wait_ge(sem(f"xnT_{k}"), b + 1)

            def prelude(k, r, b):
                norm_turn(k, b)
                for j in range(2):
                    take("proj_done", 2 * (2 * r + j) + 2)
                    pe.matmul(misc[:, :], w[k][:, j, :], xnT[k][:, :], start=True, stop=True
                              ).then_inc(sem("qk_proj"), 1)
                token_product(xnT[k], w[k][:, 2, :], "v_proj", "v_staged", r + 1)

            def s_tile(r, h, i):
                n = h * T + i
                if i == 0 and h % HG == 0:
                    pe.wait_ge(sem(f"stack_in{h // HG}"), STACK_DMAS * DMA * (r + 1))
                pe.wait_ge(sem("max_done"), H * T * r + max(n - 1, 0))
                pe.matmul(sbank[n % 2][:, :], qst[:, h, i * P:(i + 1) * P], kst[:, h, :],
                          start=True, stop=True).then_inc(sem("s_done"), 1)

            def st_item(r, n):
                g, half_, h = n // (2 * HG), n // HG % 2, n // (2 * HG) * HG + n % HG
                if n % (2 * HG) == 0:
                    pe.wait_ge(sem(f"mrow_in{g}"), PARTS * DMA * (r + 1))
                pe.wait_ge(sem("exp_done"), 2 * H * r + max(n - 1, 0))
                for c in range(2):
                    kt = 2 * half_ + c
                    last = pe.matmul(stb[n % 2][:, c, :], kst[:, h, kt * P:(kt + 1) * P], qst[:, h, :],
                                     start=True, stop=True)
                last.then_inc(sem("st_done"), 1)

            def max_rows(r, g):
                pe.wait_ge(sem("max_done"), H * T * r + (g + 1) * HG * T)
                take("max_read", G * r + g + 1)
                pe.transpose(misc[0:HG * T, 0:P], negm[:, g, :], ident[:, :]).then_inc(sem("max_T"), 1)

            def o_half(r, g, half_):
                if g == 0 and half_ == 0:
                    pe.wait_ge(sem("v_ready"), r + 1)
                pe.wait_ge(sem("exp_done"), 2 * H * r + 2 * HG * g + HG * (half_ + 1))
                if half_ == 0:
                    pe.wait_ge(sem("oT_done"), G * r + g)
                for c in range(2):
                    for j in range(HG):
                        last = pe.matmul(pv[VW * j:VW * (j + 1), :], vp[:, 2 * half_ + c, HG * g + j, :],
                                         pT[half_][:, j, c, :], start=(half_ + c == 0), stop=(half_ + c == 2))
                last.then_inc(sem("pv_done"), 1)

            def o_turn(r, g):
                pe.wait_ge(sem("oT_done"), G * r + g + 1)
                take("ctx_done", G * r + g + 1)
                for i in range(T):
                    last = pe.transpose(misc[:, i * P:(i + 1) * P], oT[:, i * P:(i + 1) * P], ident[:, :])
                last.then_inc(sem("o_turned"), 1)

            def core(r):
                for n in range(H + LAG + 2):
                    for i in range(T):
                        if n < H:
                            s_tile(r, n, i)
                        if i == 1 and n >= HG and n % HG == 0 and n // HG <= G:
                            max_rows(r, n // HG - 1)
                        if i % 2 and 0 <= n - LAG < H:
                            st_item(r, 2 * (n - LAG) + i // 2)
                    m = n - LAG - 2
                    if m >= 0 and m % 2 == 0 and m // 4 < G:
                        o_half(r, m // 4, m // 2 % 2)
                    if m >= 3 and (m - 3) % 4 == 0:
                        o_turn(r, (m - 3) // 4)

            def project(k, r, b):
                turn(ctxt, "ctx_done", G * (r + 1), f"T_ctx_{k}", f"ctxT_{k}", b + 1)
                pe.wait_ge(sem(f"ctxT_{k}"), b + 1)
                token_product(ctxT, wo[k][:, :], f"proj_{k}", f"proj_read_{k}", b + 1)

            def hidden(k, b, w_in, w_out):
                for f in range(FT):
                    take(f"act_{k}", FT * b + f + 1)
                    pe.matmul(misc[:, :], w_in[:, f * P:(f + 1) * P], xnT[k][:, :], start=True, stop=True
                              ).then_inc(sem(f"hid_{k}"), 1)
                take(f"ffn_read_{k}", b + 1)
                for i in range(T):
                    for f in range(FT):
                        last = pe.matmul(misc[:, i * P:(i + 1) * P], hT[:, f, i * P:(i + 1) * P], w_out[:, f, :],
                                         start=(f == 0), stop=(f == FT - 1))
                last.then_inc(sem(f"ffn_{k}"), 1)

            def ffn(k, b):
                norm_turn(k, b)
                take(f"srow_{k}", b + 1)
                pe.matmul(misc[:, :], wr[:, :], xnT[k][:, :], start=True, stop=True).then_inc(sem(f"score_{k}"), 1)
                hidden(k, b, w1, w2)

            def sparse(b):
                for j in range(2):
                    take("sp_qk", 2 * b + j + 1)
                    pe.matmul(misc[:, :], wqp[:, j, :], xnT["B"][:, :], start=True, stop=True
                              ).then_inc(sem("sp_proj"), 1)
                token_product(xnT["B"], wvp[:, :], "sp_v", "sp_v_in", b + 1)
                pe.wait_ge(sem("sp_qk"), 2 * (b + 1))
                for i in range(T):
                    take("sp_exp", T * b + i + 1)
                    pe.matmul(misc[:, :], qkT[:, 0, i * P:(i + 1) * P], qkT[:, 1, :], start=True, stop=True
                              ).then_inc(sem("sp_score"), 1)
                for i in range(T):
                    pe.wait_ge(sem("sp_kept"), T * b + i + 1)
                    take("sp_ET", T * b + i + 1)
                    for kt in range(T):
                        last = pe.transpose(misc[:, kt * P:(kt + 1) * P], W[:, i, kt * P:(kt + 1) * P], ident[:, :])
                    last.then_inc(sem("sp_T"), 1)
                pe.wait_ge(sem("sp_ET"), T * (b + 1))
                take("sp_out_read", b + 1)
                for i in range(T):
                    for kt in range(T):
                        last = pe.matmul(misc[:, i * P:(i + 1) * P], ET[:, i, kt, :], vsp[:, kt, :],
                                         start=(kt == 0), stop=(kt == T - 1))
                last.then_inc(sem("sp_out"), 1)

            pe.wait_ge(sem("ident_ready"), 1)
            pe.wait_ge(sem("w_in"), DMA * W_DMAS)
            pe.wait_ge(sem("wr_ready"), 1)
            pe.wait_ge(sem("stack_init"), 6)
            with pe.Fori(0, B) as b:
                bank.update(freed="ffn_read_F1", count=b)
                prelude("A", b, b)
                core(b)
                project("A", b, b)
                ffn("F1", b)
            with pe.Fori(0, B) as b:
                bank.update(freed="ffn_read_F2", count=b)
                prelude("B", b + B, b)
                sparse(b)
                core(b + B)
                project("B", b + B, b)
                turn(x1n, "x1n_ready", b + 1, "T_L1", "xnT_L1", b + 1)
                pe.wait_ge(sem("xnT_L1"), b + 1)
                hidden("L1", b, ff1, ff2)
                ffn("F2", b)

        @block.scalar
        def _(act):
            def evacuate(dst, ready, count, signal):
                act.wait_ge(sem(ready), count)
                act.activation(dst, misc[:, :], ACT.Copy).then_inc(sem(signal), 1)

            def norm_turn(k, b):
                evacuate(xnT[k][:, :], f"T_{k}", b + 1, f"xnT_{k}")

            def prelude(k, r, b):
                norm_turn(k, b)
                for j in range(2):
                    act.wait_ge(sem("qk_proj"), 2 * r + j + 1)
                    act.wait_ge(sem("parts"), 2 * r)
                    act.wait_ge(sem("parts_out"), DMA * (3 * PARTS - 1) * r)
                    act.activation(qf[:, j, :], misc[:, :], ACT.Identity, bias=colb[k][:, j:j + 1]
                                   ).then_inc(sem("proj_done"), 1)
                    act.activation(split[:, j, 0, :], misc[:, :], ACT.Identity, bias=colb[k][:, j:j + 1]
                                   ).then_inc(sem("proj_done"), 1)

            def exp_item(r, n):
                g, half_, j = n // (2 * HG), n // HG % 2, n % HG
                act.wait_ge(sem("st_done"), 2 * H * r + n + 1)
                if j == 0:
                    act.wait_ge(sem("pv_done"), 2 * G * r + max(2 * g + half_ - 1, 0))
                act.activation(pT[half_][:, j, :, :], stb[n % 2][:, :, :], ACT.Exp, scale=SCALE
                               ).then_inc(sem("exp_done"), 1)

            def core(r):
                for n in range(LAG, H + LAG + 2):
                    if n - LAG < H:
                        exp_item(r, 2 * (n - LAG))
                        exp_item(r, 2 * (n - LAG) + 1)
                    m = n - LAG - 2
                    if m >= 2 and (m - 2) % 4 == 0:
                        g = (m - 2) // 4
                        act.wait_ge(sem("pv_done"), 2 * (G * r + g + 1))
                        act.wait_ge(sem("o_turned"), G * r + g)
                        act.activation(oT[:, :], pv[:, :], ACT.Copy).then_inc(sem("oT_done"), 1)

            def hidden(k, b, func, bias):
                for f in range(FT):
                    act.wait_ge(sem(f"hid_{k}"), FT * b + f + 1)
                    act.activation(hT[:, f, :], misc[:, :], func, bias=bias[:, f:f + 1]).then_inc(sem(f"act_{k}"), 1)

            def ffn(k, b):
                norm_turn(k, b)
                evacuate(srow[:, :], f"score_{k}", b + 1, f"srow_{k}")
                act.wait_ge(sem(f"scol_{k}"), T * (b + 1))
                act.activation(gate[:, 0, :], scol[:, :], ACT.Exp, scale=-1.0).then_inc(sem(f"gate_exp_{k}"), 1)
                hidden(k, b, ACT.Gelu_apprx_tanh, col1["F"])

            def sparse(b):
                for j in range(2):
                    act.wait_ge(sem("sp_proj"), 2 * b + j + 1)
                    act.activation(qkT[:, j, :], misc[:, :], ACT.Identity, bias=colp[:, j:j + 1]
                                   ).then_inc(sem("sp_qk"), 1)
                for i in range(T):
                    act.wait_ge(sem("sp_bias"), T * b + i + 1)
                    act.activation(E[:, i, :], misc[:, :], ACT.Exp, bias=smax[:, 1, i:i + 1], scale=R ** -0.5,
                                   accum_out=sall[:, i:i + 1]).then_inc(sem("sp_exp"), 1)
                for i in range(T):
                    act.wait_ge(sem("sp_T"), T * b + i + 1)
                    act.activation(ET[:, i, :, :], misc_t, ACT.Copy).then_inc(sem("sp_ET"), 1)

            act.wait_ge(sem("w_in"), DMA * W_DMAS)
            act.activation(sig[:, 0:1], lam[:, :], ACT.Exp, scale=-1.0).then_inc(sem("lam_exp"), 1)
            with act.Fori(0, B) as b:
                prelude("A", b, b)
                core(b)
                evacuate(ctxT[:, :], "T_ctx_A", b + 1, "ctxT_A")
                ffn("F1", b)
            with act.Fori(0, B) as b:
                prelude("B", b + B, b)
                sparse(b)
                core(b + B)
                evacuate(ctxT[:, :], "T_ctx_B", b + 1, "ctxT_B")
                norm_turn("L1", b)
                hidden("L1", b, ACT.Relu, col1["L"])
                ffn("F2", b)

        @block.vector
        def _(dve):
            def norm(k, b):
                ready, unit = X_READY[k]
                dve.wait_ge(sem(ready), unit * (b + 1))
                apart(dve)
                steps = Steps(dve, f"norm_steps_{k}", b, T)
                for i in range(T):
                    steps.did(dve.bn_stats(stats[k][:, i, :], source(k, b, i)))
                steps.wait()
                apart(dve)
                for i in range(T):
                    dve.bn_aggr(mv[k][:, i, :], stats[k][:, i, :]).then_inc(sem(f"aggr_{k}"), 1)
                steps.end()
                dve.wait_ge(sem(f"rstd_{k}"), b + 1)
                for i in range(T):
                    last = dve.tensor_scalar(xn[k][:, i, :], source(k, b, i), mv[k][:, i, 0:1], rstd[k][:, i:i + 1],
                                             ALU.subtract, ALU.mult)
                last.then_inc(sem(f"xn_{k}"), 1)

            def affine(k, b, g, be, dst, ready):
                steps = Steps(dve, f"affine_steps_{k}", b, 1)
                dve.wait_ge(sem(f"xn_{k}"), b + 1)
                steps.did(dve.tensor_tensor(dst, xn[k][:, :, :], bc(g), ALU.mult))
                steps.wait()
                steps.end()
                dve.tensor_tensor(dst, dst, bc(be), ALU.add).then_inc(sem(ready), 1)

            def stage_v(r):
                dve.wait_ge(sem("v_proj"), r + 1)
                dve.wait_ge(sem("v_ready"), r)
                dve.tensor_copy(vstage[:, :, :], misc_t).then_inc(sem("v_staged"), 1)

            def max_parts(r, g):
                steps = Steps(dve, "max_steps", G * r + g, 2)
                dve.wait_ge(sem("max_T"), G * r + g + 1)
                if g == 0:
                    dve.wait_ge(sem(f"mrow_in{G - 1}"), PARTS * DMA * r)
                else:
                    dve.wait_ge(sem(f"mrow_in{g - 1}"), PARTS * DMA * (r + 1))
                rows_ = misc[0:HG * T, 0:P]
                steps.did(dve.tensor_copy(msp[:, 0, :], rows_))
                steps.wait()
                dve.tensor_tensor(mres[:, :], rows_, msp[:, 0, :], ALU.subtract).then_inc(sem("max_read"), 1)
                dve.wait_ge(sem("max_read"), G * r + g + 1)
                steps.did(dve.tensor_copy(msp[:, 1, :], mres[:, :]))
                steps.wait()
                steps.end()
                dve.tensor_tensor(msp[:, 2, :], mres[:, :], msp[:, 1, :], ALU.subtract).then_inc(sem("max_parts"), 1)

            turned = misc[:, :].rearrange("p (t j c) -> p t j c", t=T, c=VW)

            def context(r, g):
                dve.wait_ge(sem("o_turned"), G * r + g + 1)
                dve.reciprocal(rden[:, :, :, :], turned[:, :, :, DH:DH + 1]).then_inc(sem("rden"), 1)
                dve.wait_ge(sem("rden"), G * r + g + 1)
                out = ctxt[:, :, g * HG * DH:(g + 1) * HG * DH].rearrange("p t (j d) -> p t j d", d=DH)
                dve.tensor_tensor(out, turned[:, :, :, 0:DH], rden[:, :, :, :].broadcast_to([P, T, HG, DH]),
                                  ALU.mult).then_inc(sem("ctx_done"), 1)

            def core(r):
                for n in range(H + LAG + 2):
                    for i in range(T):
                        if n < H:
                            c = n * T + i
                            col = n % HG * T + i
                            dve.wait_ge(sem("s_done"), H * T * r + c + 1)
                            dve.tensor_reduce(negm[:, n // HG, col:col + 1], sbank[c % 2][:, :], AX.X, ALU.max,
                                              negate=True).then_inc(sem("max_done"), 1)
                        if i == 1 and n >= HG and n % HG == 0 and n // HG <= G:
                            max_parts(r, n // HG - 1)
                    m = n - LAG - 2
                    if m >= 3 and (m - 3) % 4 == 0:
                        context(r, (m - 3) // 4)

            def add_projection(b):
                dve.wait_ge(sem("proj_A"), b + 1)
                dve.tensor_tensor(proj[:, :, :], misc_t, bc("bo_A"), ALU.add).then_inc(sem("proj_read_A"), 1)
                dve.wait_ge(sem("proj_read_A"), b + 1)
                xb = x[:, ds(b * T, T), :]
                dve.tensor_tensor(xb, xb, proj[:, :, :], ALU.add).then_inc(sem("x_attn"), 1)

            def ffn(k, b):
                norm(k, b)
                steps = Steps(dve, f"route_steps_{k}", b, 2 * T + 3)
                dve.wait_ge(sem(f"srow_{k}"), b + 1)
                dve.wait_ge(sem(f"gate_exp_{k}"), b)
                for i in range(T):
                    dve.scalar_tensor_tensor(junk[:, i, 0:P], srow[:, i * P:(i + 1) * P], 1.0, ident[:, :],
                                             ALU.mult, ALU.mult, accum_out=scol[:, i:i + 1]
                                             ).then_inc(sem(f"scol_{k}"), 1)
                dve.wait_ge(sem(f"scol_{k}"), T * (b + 1))
                for i in range(T):
                    steps.did(dve.tensor_scalar(junk[:, i, :], srow[:, :], scol[:, i:i + 1], 0.0, ALU.is_gt, ALU.add,
                                                accum_out=rank[:, 0, i:i + 1]))
                steps.wait()
                for i in range(T):
                    steps.did(dve.scalar_tensor_tensor(junk[:, i, :], srow[:, :], scol[:, i:i + 1],
                                                       earlier[:, i, :], ALU.is_equal, ALU.mult,
                                                       accum_out=rank[:, 1, i:i + 1]))
                steps.wait()
                steps.did(dve.tensor_tensor(gate[:, 3, :], rank[:, 0, :], rank[:, 1, :], ALU.add))
                dve.wait_ge(sem(f"gate_exp_{k}"), b + 1)
                steps.did(dve.tensor_scalar(gate[:, 1, :], gate[:, 0, :], 1.0, None, ALU.add))
                steps.wait()
                steps.did(dve.reciprocal(gate[:, 2, :], gate[:, 1, :]))
                steps.wait()
                steps.end()
                dve.scalar_tensor_tensor(gate[:, 4, :], gate[:, 3, :], float(ROUTED), gate[:, 2, :],
                                         ALU.is_lt, ALU.mult).then_inc(sem(f"gate_{k}"), 1)
                dve.wait_ge(sem(f"gate_{k}"), b + 1)
                dve.wait_ge(sem(f"ffn_{k}"), b + 1)
                dve.tensor_tensor(upd[:, :, :], misc_t, bc("b2"), ALU.add).then_inc(sem(f"ffn_read_{k}"), 1)
                dve.wait_ge(sem(f"ffn_read_{k}"), b + 1)
                tail = Steps(dve, f"update_steps_{k}", b, T)
                for i in range(T):
                    tail.did(dve.scalar_tensor_tensor(upd[:, i, :], upd[:, i, :], gate[:, 4, i:i + 1], xn[k][:, i, :],
                                                      ALU.mult, ALU.add))
                tail.wait()
                tail.end()
                xb = x[:, ds(b * T, T), :]
                dve.tensor_tensor(xb, xb, upd[:, :, :], ALU.add).then_inc(sem(X_DONE[k]), 1)

            def sparse(b):
                steps = Steps(dve, "sparse_steps", b, T + 2 * T * (KEEP // 8 + 1) + 4)
                dve.wait_ge(sem("sp_v"), b + 1)
                dve.tensor_tensor(vsp[:, :, :], misc_t, bc("bvp"), ALU.add).then_inc(sem("sp_v_in"), 1)
                for i in range(T):
                    dve.wait_ge(sem("sp_score"), T * b + i + 1)
                    steps.did(dve.tensor_reduce(smax[:, 0, i:i + 1], misc[:, :], AX.X, ALU.max))
                    steps.wait()
                    dve.tensor_scalar(smax[:, 1, i:i + 1], smax[:, 0, i:i + 1], -R ** -0.5, None, ALU.mult
                                      ).then_inc(sem("sp_bias"), 1)
                dve.wait_ge(sem("sp_exp"), T * (b + 1))
                apart(dve)
                whole, rest = divmod(KEEP, 8)
                for n in range(whole + 1):
                    for i in range(T):
                        steps.did(dve.max(top[:, i, :], (W if n else E)[:, i, :]))
                    steps.wait()
                    apart(dve)
                    if n == whole:
                        steps.did(dve.memset(top[:, :, rest:8], -1.0))
                        steps.wait()
                        apart(dve)
                    for i in range(T):
                        steps.did(dve.match_replace(W[:, i, :], top[:, i, :], (W if n else E)[:, i, :], -1.0))
                    steps.wait()
                    apart(dve)
                for i in range(T):
                    dve.scalar_tensor_tensor(W[:, i, :], W[:, i, :], 0.0, E[:, i, :], ALU.is_lt, ALU.mult,
                                             accum_out=ssel[:, i:i + 1]).then_inc(sem("sp_kept"), 1)
                dve.wait_ge(sem("sp_kept"), T * (b + 1))
                steps.did(dve.scalar_tensor_tensor(rsp[:, 0, :], sall[:, :], 1e-9, ssel[:, :], ALU.mult, ALU.add))
                steps.wait()
                steps.did(dve.reciprocal(rsp[:, 1, :], rsp[:, 0, :]))
                steps.wait()
                steps.did(dve.tensor_scalar(rsp[:, 0, :], rsp[:, 1, :], sig[:, 3:4], None, ALU.mult))
                steps.wait()
                dve.wait_ge(sem("sp_out"), b + 1)
                dve.tensor_tensor(so[:, :, :], misc_t, rsp[:, 0, :].unsqueeze(2).broadcast_to([P, T, D]), ALU.mult
                                  ).then_inc(sem("sp_out_read"), 1)
                steps.end()

            def fuse(b):
                dve.wait_ge(sem("proj_B"), b + 1)
                dve.tensor_tensor(proj[:, :, :], misc_t, bc("bo_B"), ALU.add).then_inc(sem("proj_read_B"), 1)
                dve.wait_ge(sem("proj_read_B"), b + 1)
                dve.wait_ge(sem("sp_out_read"), b + 1)
                steps = Steps(dve, "fuse_steps", b, 1)
                steps.did(dve.scalar_tensor_tensor(proj[:, :, :], proj[:, :, :], sig[:, 2:3], so[:, :, :],
                                                   ALU.mult, ALU.add))
                steps.wait()
                steps.end()
                dve.tensor_tensor(x1[:, :, :], proj[:, :, :], xn["B"][:, :, :], ALU.add).then_inc(sem("x1_ready"), 1)

            def layer_ffn(b):
                norm("L1", b)
                affine("L1", b, "g1", "be1", x1n[:, :, :], "x1n_ready")
                dve.wait_ge(sem("x1n_ready"), b + 1)
                dve.wait_ge(sem("ffn_L1"), b + 1)
                dve.tensor_tensor(y1[:, :, :], misc_t, bc("ff2b"), ALU.add).then_inc(sem("ffn_read_L1"), 1)
                dve.wait_ge(sem("ffn_read_L1"), b + 1)
                dve.tensor_tensor(y1[:, :, :], y1[:, :, :], x1n[:, :, :], ALU.add).then_inc(sem("y1_ready"), 1)
                norm("L2", b)
                affine("L2", b, "g2", "be2", proj[:, :, :], "y_ready")
                dve.wait_ge(sem("y_ready"), b + 1)
                xb = x[:, ds(b * T, T), :]
                dve.tensor_tensor(xb, xb, proj[:, :, :], ALU.add).then_inc(sem("x_layer"), 1)

            dve.memset(qst[:, :, :], 0.0).then_inc(sem("stack_init"), 1)
            dve.memset(kst[:, :, :], 0.0).then_inc(sem("stack_init"), 1)
            dve.memset(vp[:, :, :, :], 0.0).then_inc(sem("stack_init"), 1)
            dve.memset(zrows[:, :], 0.0).then_inc(sem("stack_init"), 1)
            dve.wait_ge(sem("stack_init"), 4)
            dve.memset(kst[MROW:MROW + PARTS, :, :], 1.0).then_inc(sem("stack_init"), 1)
            dve.memset(vp[:, :, :, DH:DH + 1], 1.0).then_inc(sem("stack_init"), 1)
            dve.wait_ge(sem("w_in"), DMA * W_DMAS)
            dve.wait_ge(sem("ident_ready"), 1)
            dve.wait_ge(sem("earlier_ready"), 1)
            dve.tensor_copy(wr[:, :], wr_col[:, :].broadcast_to([P, P])).then_inc(sem("wr_ready"), 1)
            dve.wait_ge(sem("lam_exp"), 1)
            dve.tensor_scalar(sig[:, 1:2], sig[:, 0:1], 1.0, None, ALU.add).then_inc(sem("sig_steps"), 1)
            dve.wait_ge(sem("sig_steps"), 1)
            dve.reciprocal(sig[:, 2:3], sig[:, 1:2]).then_inc(sem("sig_steps"), 1)
            dve.wait_ge(sem("sig_steps"), 2)
            dve.tensor_scalar(sig[:, 3:4], sig[:, 2:3], -1.0, 1.0, ALU.mult, ALU.add).then_inc(sem("sig_steps"), 1)
            dve.wait_ge(sem("sig_steps"), 3)
            with dve.Fori(0, B) as b:
                norm("A", b)
                stage_v(b)
                core(b)
                add_projection(b)
                ffn("F1", b)
            with dve.Fori(0, B) as b:
                norm("B", b)
                stage_v(b + B)
                sparse(b)
                core(b + B)
                fuse(b)
                layer_ffn(b)
                ffn("F2", b)


def kernel(**inputs):
    import concourse.bacc as bacc
    from concourse.bass_utils import run_bass_kernel_spmd

    a = {k: np.asarray(v) for k, v in inputs.items()}
    m = np.arange(D)

    def circulant(name):
        return a[name][(m[None, :] - m[:, None]) % D]

    A, L = "L0_attn_a_", "L0_attn_b_"
    arrays = {
        "x": a[A + "x"].reshape(B * SEQ, D),
        "w_A": np.stack([circulant(f"{A}w{n}_c") for n in "qkv"], 1),
        "wo_A": circulant(A + "wo_c"),
        "b_A": np.concatenate([a[f"{A}w{n}_b"] for n in "qkv"]),
        "bo_A": a[A + "wo_b"],
        "w_B": a[L + "in_proj_w"].T.reshape(D, 3, D),
        "wo_B": a[L + "out_proj_w"].T,
        "b_B": a[L + "in_proj_b"],
        "bo_B": a[L + "out_proj_b"],
        "QpT": a[L + "Qp_w"].T, "Qpb": a[L + "Qp_b"],
        "KpT": a[L + "Kp_w"].T, "Kpb": a[L + "Kp_b"],
        "VpT": a[L + "Vp_w"].T, "Vpb": a[L + "Vp_b"],
        "lam": a[L + "lam"].reshape(1),
        "ff1T": a[L + "ff1_w"].T, "ff1b": a[L + "ff1_b"].reshape(FT, P).T,
        "ff2T": a[L + "ff2_w"].T, "ff2b": a[L + "ff2_b"],
        "ln1g": a[L + "ln1_g"], "ln1b": a[L + "ln1_b"], "ln2g": a[L + "ln2_g"], "ln2b": a[L + "ln2_b"],
        "wr": a["L0_ffn_w_router"], "W1": a["L0_ffn_W1"], "b1": a["L0_ffn_b1"].reshape(FT, P).T,
        "W2": a["L0_ffn_W2"], "b2": a["L0_ffn_b2"],
    }
    arrays = {k: np.ascontiguousarray(v) for k, v in arrays.items()}
    nc = bacc.Bacc("TRN2", target_bir_lowering=False, num_devices=1)
    t = {k: nc.dram_tensor(f"in_{k}", v.shape, F32, kind="ExternalInput").ap() for k, v in arrays.items()}
    t["out"] = nc.dram_tensor("out", (B * SEQ, D), F32, kind="ExternalOutput").ap()
    build(nc, t)
    r = run_bass_kernel_spmd(nc, [{f"in_{k}": v for k, v in arrays.items()}], core_ids=[0])
    return r.results[0]["out"].reshape(B, SEQ, D)
```

```python
from contextlib import ExitStack

import numpy as np
import concourse.bass as bass
import concourse.mybir as mybir
from concourse.alu_op_type import AluOpType as ALU

ACT = mybir.ActivationFunctionType
AX = mybir.AxisListType
F32 = mybir.dt.float32
BF16 = mybir.dt.bfloat16
ds = bass.ds

P = 128
B, SEQ, D = 4, 512, 128
T = SEQ // P
H, DH = 16, 8
G = 4
HG = H // G
IDLES = 128
PARTS = 3
SLOT = PARTS * DH
MROW = 96
VW = 32
FF = 512
FT = FF // P
R = 64
KEEP = int(SEQ * 0.2)
ROUTED = SEQ // 2
LAG = 6
TINY = -2.0 ** -126
EPS = 1e-5
SCALE = DH ** -0.5
DMA = 16
STACK_DMAS = 7


def build(nc, t):
    with ExitStack() as ctx:
        def sb(name, shape, dt=F32):
            return ctx.enter_context(nc.sbuf_tensor(name, shape, dt))

        def ps(name, shape, dt=F32):
            return ctx.enter_context(nc.psum_tensor(name, shape, dt))

        sems = {}

        def sem(name):
            if name not in sems:
                sems[name] = ctx.enter_context(nc.semaphore(name))
            return sems[name]

        ident = sb("ident", [P, P])
        earlier = sb("earlier", [P, T, SEQ], BF16)
        w = {k: sb(f"w_{k}", [P, 3, P]) for k in "AB"}
        wo = {k: sb(f"wo_{k}", [P, P]) for k in "AB"}
        wr_col = sb("wr_col", [P, 1])
        wr = sb("wr", [P, P])
        w1 = sb("w1", [P, FF])
        w2 = sb("w2", [P, FT, D])
        ff1 = sb("ff1", [P, FF])
        ff2 = sb("ff2", [P, FT, D])
        wqp = sb("wqp", [P, 2, P])
        wvp = sb("wvp", [P, P])
        colb = {k: sb(f"colb_{k}", [P, 2]) for k in "AB"}
        colp = sb("colp", [P, 2])
        col1 = {"F": sb("col_b1", [P, FT]), "L": sb("col_ff1b", [P, FT])}
        rows = {}
        bv = sb("bv", [P, 2, P])
        for name in ("bo_A", "bo_B", "bvp", "b2", "ff2b", "g1", "be1", "g2", "be2"):
            rows[name] = sb(f"row_{name}", [P, P])
        lam = sb("lam", [P, 1])
        sig = sb("sig", [P, 4])
        half = sb("half", [P, T])
        eps = sb("eps", [P, T])
        idle = sb("idle", [1, IDLES])

        x = sb("x", [P, B * T, D])
        LNS = ("A", "F1", "B", "L1", "L2", "F2")
        stats = {k: sb(f"stats_{k}", [P, T, 6]) for k in LNS}
        mv = {k: sb(f"mv_{k}", [P, T, 2]) for k in LNS}
        vare = {k: sb(f"vare_{k}", [P, T]) for k in LNS}
        rstd = {k: sb(f"rstd_{k}", [P, T]) for k in LNS}
        xn = {k: sb(f"xn_{k}", [P, T, D]) for k in LNS if k != "B"}
        xnT = {"A": sb("xnT_att", [P, SEQ]), "F1": sb("xnT_ffn", [P, SEQ])}
        xnT.update(B=xnT["A"], L1=xnT["F1"], F2=xnT["F1"])

        qf = sb("qf", [P, 2, SEQ])
        qr = sb("qr", [P, SEQ])
        split = sb("split", [P, 2, PARTS, SEQ], BF16)
        qst = sb("qst", [P, H, SEQ], BF16)
        kst = sb("kst", [P, H, SEQ], BF16)
        zrows = sb("zrows", [PARTS, SEQ], BF16)
        vstage = sb("vstage", [P, T, D])
        vp = sb("vp", [P, T, H, VW])
        negm = sb("negm", [P, G, HG * T])
        mres = sb("mres", [HG * T, P])
        msp = sb("msp", [HG * T, PARTS, P], BF16)
        pT = [sb(f"pT{n}", [P, HG, 2, SEQ]) for n in range(2)]
        oT = sb("oT", [P, SEQ])
        rden = sb("rden", [P, T, HG, 1])
        ctxt = sb("ctxt", [P, T, D])
        ctxT = sb("ctxT", [P, SEQ])
        proj = sb("proj", [P, T, D])

        srow = sb("srow", [P, SEQ])
        junk = sb("junk", [P, T, SEQ], BF16)
        scol = sb("scol", [P, T])
        rank = sb("rank", [P, T])
        gate = sb("gate", [P, 4, T])
        hT = sb("hT", [P, FT, SEQ])
        upd = sb("upd", [P, T, D])

        qkT = sb("qkT", [P, 2, SEQ])
        vsp = sb("vsp", [P, T, D])
        smax = sb("smax", [P, 2, T])
        E = sb("E", [P, T, SEQ])
        W = sb("W", [P, T, SEQ])
        top8 = sb("top8", [P, T, 8])
        sall = sb("sall", [P, T])
        ssel = sb("ssel", [P, T])
        rsp = sb("rsp", [P, 2, T])
        ET = E[:, :, :].rearrange("p t (k q) -> p t k q", q=P)
        base = sb("base", [P, B * T, D])
        x1 = sb("x1", [P, T, D])
        x1n = sb("x1n", [P, T, D])
        y1 = sb("y1", [P, T, D])

        sbank = [ps(f"sbank{n}", [P, SEQ]) for n in range(2)]
        stb = [ps(f"stb{n}", [P, 2, SEQ]) for n in range(2)]
        pv = ps("pv", [P, SEQ])
        misc = ps("misc", [P, SEQ])
        misc_t = misc[:, :].rearrange("p (t d) -> p t d", t=T)

        qd = nc.dram_tensor("q_parts", (H, PARTS, DH, SEQ), BF16, kind="Internal").ap()
        kd = nc.dram_tensor("k_parts", (H, 2 * PARTS - 1, DH, SEQ), BF16, kind="Internal").ap()
        x_tiles = t["x"].rearrange("(t p) d -> p t d", p=P)
        o_tiles = t["out"].rearrange("(t p) d -> p t d", p=P)

        def later(count):
            return not isinstance(count, int) or count > 0

        class Steps:

            def __init__(self, eng, name, b, n, k=0):
                self.eng, self.name, self.base, self.n, self.k = eng, name, b * n, n, k

            def did(self, ins):
                ins.then_inc(sem(self.name), 1)
                self.k += 1

            def wait(self):
                self.eng.wait_ge(sem(self.name), self.base + self.k)

            def end(self):
                assert self.k == self.n, (self.k, self.n)

        def apart(dve, count):
            if not isinstance(count, int):
                place = idle_at.pop()
                dve.memset(idle[:, place:place + 1], 0.0)

        idle_at = list(range(IDLES))

        block = ctx.enter_context(nc.Block())

        X_READY = {"F1": ("x_attn", 1), "B": ("x_ffn1", 1), "L1": ("x1_ready", 1),
                   "L2": ("y1_ready", 1), "F2": ("x_layer", 1)}
        X_DONE = {"F1": "x_ffn1", "F2": "x_ffn2"}

        def batch(b, of=x):
            return of[:, b * T:(b + 1) * T, :] if isinstance(b, int) else of[:, ds(b * T, T), :]

        def source(k, b, i):
            if k == "L1":
                return x1[:, i, :]
            if k == "L2":
                return y1[:, i, :]
            return x[:, b * T + i, :] if isinstance(b, int) else x[:, ds(b * T + i, 1), :]

        def bc(row):
            return rows[row][:, :].unsqueeze(1).broadcast_to([P, T, D])

        def kind(r):
            return ("A", 0) if r < B else ("B", B)

        def prelude(k, first):
            return [(0, "stats", k, first), (2, "apply", k, first), (5, "turn", k, first),
                    (7, "project_q", k, first), (9, "project_k", k, first), (35, "project_v", k, first)]

        def sparse(first):
            at = 28
            topk = [(at + n, "top", n, first) for n in range(4 * (KEEP // 8 + 1))]
            after = at + len(topk)
            return ([(13, "sparse_q", "B", first), (15, "sparse_k", "B", first), (23, "sparse_v", "B", first)]
                    + [(at - T + i, "sparse_score", i, first) for i in range(T)] + topk
                    + [(after, "sparse_keep", "B", first)]
                    + [(after + 1 + i // 2, "sparse_turn", i, first) for i in range(T)]
                    + [(after + 3 + i, f"sparse_out{i}", "B", first) for i in range(T)])

        def out_projection(k, first, at):
            return [(at, "turn_context", k, first), (at + 2, "project_out", k, first)]

        def norm_turned(k, first, at):
            return [(at, "stats", k, first), (at + 2, "apply", k, first), (at + 5, "turn", k, first)]

        def hidden(k, first, at, spacing, out):
            gelu = [] if k == "L1" else [(at + spacing * (FT - 1), "gelu", k, first)]
            return ([(at + spacing * f, f"hidden{f}", k, first) for f in range(FT)] + gelu
                    + [(out + i, f"ffn_out{i}", k, first) for i in range(T)])

        def ffn(k, first, at, spacing, out):
            return (norm_turned(k, first, at) + [(at + 7, "score", k, first)] + hidden(k, first, at + 8, spacing, out)
                    + [(at + 9, "own_score", k, first), (at + 11, "rank", k, first), (out + T, "update", k, first)])

        def layer_ffn(first, at, out):
            return (norm_turned("L1", first, at) + hidden("L1", first, at + 7, 1, out)
                    + [(out + T + 1, "stats", "L2", first), (out + T + 3, "apply", "L2", first)])

        STEPS = H * T
        ROUNDS = 2 * B

        def sides(r):
            out = []
            if r + 1 < ROUNDS:
                k, first = kind(r + 1)
                out += prelude(k, first - 1)
                if k == "B":
                    out += [piece for piece in sparse(first - 1) if piece[0] < STEPS]
            if B <= r < ROUNDS:
                out += [(step - STEPS, name, arg, behind) for step, name, arg, behind in sparse(B)
                        if step >= STEPS]
            if 0 < r < ROUNDS:
                k, first = kind(r - 1)
                out += out_projection(k, first + 1, 32)
                out += layer_ffn(first + 1, 36, 50) if k == "B" else ffn("F1", first + 1, 36, 2, 58)
            if B + 2 <= r < ROUNDS:
                out += ffn("F2", B + 2, 5, 1, 27)
            if r < ROUNDS:
                out += [(28, "place_v", r, 0)]
            if r == ROUNDS:
                out += ffn("F2", B + 2, 1, 2, 24) + out_projection("B", B + 1, 32) + layer_ffn(B + 1, 36, 49)
                out += ffn("F2", B + 1, 64, 2, 90)
            by_step = {}
            for piece in sorted(out, key=lambda x: x[0]):
                by_step.setdefault(min(piece[0], STEPS - 2) if r < ROUNDS else piece[0], []).append(piece[1:])
            return by_step

        def lagging(like, n, lag):
            return like > 0 and n < lag or like < ROUNDS and n >= lag

        def hidden_bank(r, f):
            return sbank[f % 2] if isinstance(r, int) and r == ROUNDS else misc

        def run(eng, core, piece):
            def period(like, r):
                by_step = sides(like)
                for step in range(max(STEPS, max(by_step) + 1)):
                    n, i = divmod(step, T)
                    if step < STEPS:
                        core(like, r, n, i)
                    for name, arg, behind in by_step.get(step, ()):
                        piece(name, arg, r, r - behind)

            for _, name, arg, _ in prelude("A", 0):
                piece(name, arg, -1, 0)
            period(0, 0)
            with eng.Fori(1, B - 1) as r:
                period(1, r)
            for r in range(B - 1, ROUNDS + 1):
                period(r, r)

        @block.sync
        def _(sp):
            def load(dst, src, name):
                sp.dma_start(dst, src).then_inc(sem(name), DMA)

            load(x[:, 0:T, :], x_tiles[:, 0:T, :], "x_first")
            for k in "AB":
                name = "w_first" if k == "A" else "w_in"
                load(w[k][:, :, :], t[f"w_{k}"], name)
                for j in range(2):
                    load(colb[k][:, j:j + 1], t[f"b_{k}"][j * D:(j + 1) * D].unsqueeze(1), name)
                load(bv[:, int(k == "B"), :], t[f"b_{k}"][2 * D:3 * D].partition_broadcast(P), name)
                if k == "A":
                    load(x[:, T:B * T, :], x_tiles[:, T:B * T, :], "x_in")
                load(wo[k][:, :], t[f"wo_{k}"], "w_in")
                load(rows[f"bo_{k}"][:, :], t[f"bo_{k}"].partition_broadcast(P), "w_in")
            load(wr_col[:, :], t["wr"].unsqueeze(1), "w_in")
            load(w1[:, :], t["W1"], "w_in")
            load(w2[:, :, :], t["W2"].rearrange("(f p) d -> p f d", p=P), "w_in")
            load(ff1[:, :], t["ff1T"], "w_in")
            load(ff2[:, :, :], t["ff2T"].rearrange("(f p) d -> p f d", p=P), "w_in")
            sp.wait_ge(sem("zeros"), 2)
            for j, k in enumerate("QK"):
                load(wqp[:, j, 0:R], t[f"{k}pT"], "w_in")
                load(colp[0:R, j:j + 1], t[f"{k}pb"].unsqueeze(1), "w_in")
            load(wvp[:, :], t["VpT"], "w_in")
            load(col1["F"][:, :], t["b1"], "w_in")
            load(col1["L"][:, :], t["ff1b"], "w_in")
            for row, name in (("bvp", "Vpb"), ("b2", "b2"), ("ff2b", "ff2b"), ("g1", "ln1g"), ("be1", "ln1b"),
                              ("g2", "ln2g"), ("be2", "ln2b")):
                load(rows[row][:, :], t[name].partition_broadcast(P), "w_in")
            load(lam[:, :], t["lam"].partition_broadcast(P), "w_in")

            def value(v):
                return v if isinstance(v, int) else sp.snap(v)

            def store_parts(at, r):
                sp.wait_ge(sem("parts"), at["split"])
                for g in range(G):
                    if later(at["restacked"]):
                        sp.wait_ge(sem(f"stack_in{g}"), at["restacked"])
                for s in range(PARTS):
                    sp.dma_start(qd[:, s, :, :], split[:, 0, s, :]).then_inc(sem("parts_out"), DMA)
                for s in range(2 * PARTS - 1):
                    sp.dma_start(kd[:, s, :, :], split[:, 1, s % PARTS, :]).then_inc(sem("parts_out"), DMA)
                sp.wait_ge(sem("parts_out"), at["stored"])

            def fill_stacks(g, st_over):
                heads = slice(g * HG, (g + 1) * HG)
                if later(st_over):
                    sp.wait_ge(sem("st_done"), st_over)
                done = sem(f"stack_in{g}")
                for n, first in enumerate((0, 2, 1)):
                    lines = slice(n * SLOT, (n + 1) * SLOT)
                    sp.dma_start(qst[lines, heads, :], qd[heads, :, :, :].rearrange("h s d t -> (s d) h t")
                                 ).then_inc(done, DMA)
                    sp.dma_start(kst[lines, heads, :],
                                 kd[heads, first:first + PARTS, :, :].rearrange("h s d t -> (s d) h t")
                                 ).then_inc(done, DMA)
                sp.dma_start(qst[MROW:MROW + PARTS, heads, :],
                             zrows[:, :].unsqueeze(1).broadcast_to([PARTS, HG, SEQ])).then_inc(done, DMA)

            def fill_max(g, split_):
                sp.wait_ge(sem("max_parts"), split_)
                for s in range(PARTS):
                    sp.dma_start(qst[MROW + s:MROW + s + 1, g * HG:(g + 1) * HG, :], msp[:, s, :]
                                 ).then_inc(sem(f"mrow_in{g}"), DMA)

            def store_x(b):
                sp.wait_ge(sem("x_ffn2"), b + 1)
                sp.dma_start(o_tiles[:, b * T:(b + 1) * T, :], batch(b)).then_inc(sem("out"), DMA)

            def next_parts(r):
                return {"split": value(2 * r + 2), "restacked": value(STACK_DMAS * r * DMA),
                        "stored": value(DMA * (3 * PARTS - 1) * (r + 1))}

            def group_values(r):
                over = [value(r * H * 2 + 2 * HG * (g + 1) - 2 * H) for g in range(G)]
                return over, [value(G * r + g + 1) for g in range(G)]

            def period(like, r):
                over, parts = group_values(r)
                if like > 0:
                    fill_max(G - 1, value(G * r))
                if like < ROUNDS:
                    fill_stacks(2, over[2])
                    fill_max(0, parts[0])
                    fill_stacks(3, over[3])
                    fill_max(1, parts[1])
                    if like + 1 < ROUNDS:
                        store_parts(next_parts(r + 1), r + 1)
                        over, _ = group_values(r + 1)
                        fill_stacks(0, over[0])
                        fill_max(2, parts[2])
                        fill_stacks(1, over[1])
                    else:
                        fill_max(2, parts[2])
                if like > B + 1:
                    store_x(like - B - 2)

            store_parts(next_parts(0), 0)
            sp.wait_ge(sem("stack_init"), 6)
            fill_stacks(0, 0)
            fill_stacks(1, 0)
            period(0, 0)
            with sp.Fori(1, B - 1) as r:
                period(1, r)
            for r in range(B - 1, ROUNDS + 1):
                period(r, r)
            store_x(B - 1)
            sp.wait_ge(sem("out"), DMA * B)

        W_FIRST = 4
        W_DMAS = 2 * 6 - W_FIRST + 5 + 4 + 3 + 7 + 1

        @block.gpsimd
        def _(pool):
            pool.memset(half[:, :], -0.5).then_inc(sem("pool_init"), 1)
            pool.memset(eps[:, :], EPS).then_inc(sem("pool_init"), 1)
            pool.memset(ident[:, :], 0.0).then_inc(sem("pool_init"), 1)
            pool.wait_ge(sem("pool_init"), 3)
            pool.affine_select(out=ident[:, :], in_=ident[:, :], compare_op=ALU.not_equal, fill=1.0, base=0,
                               pattern=[[-1, P]], channel_multiplier=1).then_inc(sem("ident_ready"), 1)

            def rest_of_setup():
                pool.memset(wqp[:, :, :], 0.0).then_inc(sem("zeros"), 1)
                pool.memset(colp[:, :], 0.0).then_inc(sem("zeros"), 1)
                pool.memset(earlier[:, :, :], TINY).then_inc(sem("pool_init"), 1)
                pool.wait_ge(sem("pool_init"), 4)
                pool.affine_select(out=earlier[:, :, :], in_=earlier[:, :, :], compare_op=ALU.is_gt, fill=0.0, base=0,
                                   pattern=[[P, T], [-1, SEQ]], channel_multiplier=1
                                   ).then_inc(sem("earlier_ready"), 1)

            def rstds(k, b):
                pool.wait_ge(sem(f"aggr_{k}"), T * (b + 1))
                pool.tensor_tensor(vare[k][:, :], mv[k][:, :, 1], eps[:, :], ALU.add).then_inc(sem(f"vare_{k}"), 1)
                pool.wait_ge(sem(f"vare_{k}"), b + 1)
                pool.tensor_tensor(rstd[k][:, :], vare[k][:, :], half[:, :], ALU.pow).then_inc(sem(f"rstd_{k}"), 1)

            def parts(r, j):
                steps = Steps(pool, "split_steps", 2 * r + j, 2)
                if later(2 * r + j):
                    pool.wait_ge(sem("parts"), 2 * r + j)
                pool.wait_ge(sem("proj_done"), 2 * (2 * r + j) + 2)
                if later(DMA * (3 * PARTS - 1) * r):
                    pool.wait_ge(sem("parts_out"), DMA * (3 * PARTS - 1) * r)
                steps.did(pool.tensor_tensor(qr[:, :], qf[:, j, :], split[:, j, 0, :], ALU.subtract))
                steps.did(pool.tensor_tensor(split[:, j, 1, :], qf[:, j, :], split[:, j, 0, :], ALU.subtract))
                steps.wait()
                steps.end()
                pool.tensor_tensor(split[:, j, 2, :], qr[:, :], split[:, j, 1, :], ALU.subtract
                                   ).then_inc(sem("parts"), 1)

            def place_v(like, r):
                bias = bv[:, ds(int(like >= B), 1), :].broadcast_to([P, T, D])
                pool.wait_ge(sem("v_staged"), r + 1)
                if isinstance(r, int) and r == 0:
                    pool.wait_ge(sem("stack_init"), 6)
                if later(2 * G * r):
                    pool.wait_ge(sem("pv_done"), 2 * G * r)
                pool.tensor_tensor(vp[:, :, :, 0:DH], vstage[:, :, :].rearrange("p t (h d) -> p t h d", h=H),
                                   bias.rearrange("p t (h d) -> p t h d", h=H), ALU.add
                                   ).then_inc(sem("v_ready"), 1)

            def core(like, r, n, i):
                pass

            def piece(name, arg, r, b):
                if name == "stats":
                    rstds(arg, b)
                elif name == "project_q":
                    parts(r + 1, 0)
                elif name == "project_k":
                    parts(r + 1, 1)
                    if isinstance(r, int) and r == -1:
                        rest_of_setup()
                elif name == "place_v":
                    place_v(arg, r)

            pool.wait_ge(sem("w_first"), DMA * W_FIRST)
            run(pool, core, piece)

        @block.tensor
        def _(pe):
            bank = {"freed": None, "count": 0}

            def take(freed, count):
                if bank["freed"]:
                    pe.wait_ge(sem(bank["freed"]), bank["count"])
                bank.update(freed=freed, count=count)

            def turn(src, ready, count, signal, freed, freed_count):
                pe.wait_ge(sem(ready), count)
                take(freed, freed_count)
                for i in range(T):
                    last = pe.transpose(misc[:, i * P:(i + 1) * P], src[:, i, :], ident[:, :])
                last.then_inc(sem(signal), 1)

            def token_product(lhsT, rhs, signal, freed, count):
                take(freed, count)
                for i in range(T):
                    last = pe.matmul(misc[:, i * P:(i + 1) * P], lhsT[:, i * P:(i + 1) * P], rhs,
                                     start=True, stop=True)
                last.then_inc(sem(signal), 1)

            def s_tile(r, h, i):
                n = h * T + i
                if i == 0 and h % HG == 0:
                    pe.wait_ge(sem(f"stack_in{h // HG}"), STACK_DMAS * DMA * (r + 1))
                if later(H * T * r + n - 1):
                    pe.wait_ge(sem("max_done"), H * T * r + n - 1)
                pe.matmul(sbank[n % 2][:, :], qst[:, h, i * P:(i + 1) * P], kst[:, h, :],
                          start=True, stop=True).then_inc(sem("s_done"), 1)

            def st_item(r, n):
                g, half_, h = n // (2 * HG), n // HG % 2, n // (2 * HG) * HG + n % HG
                if n % (2 * HG) == 0:
                    pe.wait_ge(sem(f"mrow_in{g}"), PARTS * DMA * (r + 1))
                if later(2 * H * r + n - 1):
                    pe.wait_ge(sem("exp_done"), 2 * H * r + n - 1)
                for c in range(2):
                    kt = 2 * half_ + c
                    last = pe.matmul(stb[n % 2][:, c, :], kst[:, h, kt * P:(kt + 1) * P], qst[:, h, :],
                                     start=True, stop=True)
                last.then_inc(sem("st_done"), 1)

            def max_rows(r, g):
                pe.wait_ge(sem("max_done"), H * T * r + (g + 1) * HG * T)
                take("max_read", G * r + g + 1)
                pe.transpose(misc[0:HG * T, 0:P], negm[:, g, :], ident[:, :]).then_inc(sem("max_T"), 1)

            def o_quarter(r, g, half_, c):
                if g == 0 and half_ == 0 and c == 0:
                    pe.wait_ge(sem("v_ready"), r + 1)
                pe.wait_ge(sem("exp_done"), 2 * H * r + 2 * HG * g + HG * (half_ + 1))
                if half_ == 0 and c == 0:
                    if later(G * r + g):
                        pe.wait_ge(sem("oT_done"), G * r + g)
                for j in range(HG):
                    last = pe.matmul(pv[VW * j:VW * (j + 1), :], vp[:, 2 * half_ + c, HG * g + j, :],
                                     pT[half_][:, j, c, :], start=(2 * half_ + c == 0),
                                     stop=(2 * half_ + c == T - 1))
                if c:
                    last.then_inc(sem("pv_done"), 1)

            def o_turn(r, g):
                pe.wait_ge(sem("oT_done"), G * r + g + 1)
                take("ctx_done", G * r + g + 1)
                for i in range(T):
                    last = pe.transpose(misc[:, i * P:(i + 1) * P], oT[:, i * P:(i + 1) * P], ident[:, :])
                last.then_inc(sem("o_turned"), 1)

            def core(like, r, n, i):
                if n == 0 and i == 0 and like > 0:
                    bank.update(freed="ctx_done", count=G * (r - 1) + 2)
                if n == 0 and i == 0 and like == 0:
                    pe.wait_ge(sem("stack_init"), 6)
                    pe.wait_ge(sem("w_in"), DMA * W_DMAS)
                    pe.wait_ge(sem("wr_ready"), 1)
                if like < ROUNDS:
                    s_tile(r, n, i)
                if i == 1 and n % HG == 0 and (n > 0 or like > 0) and (n == 0 or like < ROUNDS):
                    max_rows(*((r, n // HG - 1) if n else (r - 1, G - 1)))
                if i % 2 and lagging(like, n, LAG):
                    st_item(r if n >= LAG else r - 1, 2 * ((n - LAG) % H) + i // 2)
                if lagging(like, n, LAG + 2):
                    m, r_ = (n - LAG - 2) % H, r if n >= LAG + 2 else r - 1
                    if (m % 2, i) in ((0, 2), (1, 0)):
                        o_quarter(r_, m // 4, m // 2 % 2, m % 2)
                    if (m % 4, i) == (3, T - 1):
                        o_turn(r_, m // 4)

            def piece(name, k, r, b):
                if name in ("stats", "update", "rank", "place_v", "gelu", "top", "sparse_keep"):
                    return
                if name == "turn":
                    ready = "x1n_ready" if k == "L1" else f"xn_{k}"
                    src = x1n if k == "L1" else batch(b, base) if k == "B" else xn[k]
                    turn(src, ready, b + 1, f"T_{k}", f"xnT_{k}", b + 1)
                elif name in ("project_q", "project_k"):
                    j = int(name == "project_k")
                    pe.wait_ge(sem(f"xnT_{k}"), b + 1)
                    take("proj_done", 2 * (2 * (r + 1) + j) + 2)
                    pe.matmul(misc[:, :], w[k][:, j, :], xnT[k][:, :], start=True, stop=True
                              ).then_inc(sem("qk_proj"), 1)
                elif name == "project_v":
                    token_product(xnT[k], w[k][:, 2, :], "v_proj", "v_staged", r + 2)
                elif name == "turn_context":
                    turn(ctxt, "ctx_done", G * r, f"T_ctx_{k}", f"ctxT_{k}", b + 1)
                elif name == "project_out":
                    pe.wait_ge(sem(f"ctxT_{k}"), b + 1)
                    token_product(ctxT, wo[k][:, :], f"proj_{k}", f"proj_read_{k}", b + 1)
                elif name == "score":
                    pe.wait_ge(sem(f"xnT_{k}"), b + 1)
                    take(f"srow_{k}", b + 1)
                    pe.matmul(misc[:, :], wr[:, :], xnT[k][:, :], start=True, stop=True
                              ).then_inc(sem(f"score_{k}"), 1)
                elif name == "own_score":
                    turn(srow[:, :].rearrange("p (t q) -> p t q", t=T), f"srow_{k}", b + 1, f"T_own_{k}",
                         f"gate_exp_{k}", b + 1)
                elif name.startswith("hidden"):
                    f = int(name[6:])
                    pe.wait_ge(sem(f"xnT_{k}"), b + 1)
                    bank_ = hidden_bank(r, f)
                    if bank_ is misc:
                        take(f"act_{k}", FT * b + f + 1)
                    elif f < 2:
                        pe.wait_ge(sem("max_done"), H * T * ROUNDS)
                    else:
                        pe.wait_ge(sem(f"act_{k}"), FT * b + f - 1)
                    w_in = ff1 if k == "L1" else w1
                    pe.matmul(bank_[:, :], w_in[:, f * P:(f + 1) * P], xnT[k][:, :], start=True, stop=True
                              ).then_inc(sem(f"hid_{k}"), 1)
                elif name.startswith("ffn_out"):
                    i = int(name[7:])
                    if i == 0:
                        pe.wait_ge(sem(f"act_{k}"), FT * (b + 1))
                        if k != "L1":
                            pe.wait_ge(sem(f"gelu_{k}"), b + 1)
                        take(f"ffn_read_{k}", b + 1)
                    assert bank["freed"] == f"ffn_read_{k}", "the shared bank is taken"
                    w_out = ff2 if k == "L1" else w2
                    for f in range(FT):
                        last = pe.matmul(misc[:, i * P:(i + 1) * P], hT[:, f, i * P:(i + 1) * P],
                                         w_out[:, f, :], start=(f == 0), stop=(f == FT - 1))
                    if i == T - 1:
                        last.then_inc(sem(f"ffn_{k}"), 1)
                elif name in ("sparse_q", "sparse_k"):
                    j = int(name == "sparse_k")
                    take("sp_qk", 2 * b + j + 1)
                    pe.matmul(misc[:, :], wqp[:, j, :], xnT["B"][:, :], start=True, stop=True
                              ).then_inc(sem("sp_proj"), 1)
                elif name == "sparse_v":
                    token_product(xnT["B"], wvp[:, :], "sp_v", "sp_v_in", b + 1)
                elif name == "sparse_score":
                    pe.wait_ge(sem("sp_qk"), 2 * (b + 1))
                    take("sp_exp", T * b + k + 1)
                    pe.matmul(misc[:, :], qkT[:, 0, k * P:(k + 1) * P], qkT[:, 1, :], start=True, stop=True
                              ).then_inc(sem("sp_score"), 1)
                elif name == "sparse_turn":
                    pe.wait_ge(sem("sp_kept"), T * b + k + 1)
                    take("sp_ET", T * b + k + 1)
                    for kt in range(T):
                        last = pe.transpose(misc[:, kt * P:(kt + 1) * P], W[:, k, kt * P:(kt + 1) * P], ident[:, :])
                    last.then_inc(sem("sp_T"), 1)
                elif name.startswith("sparse_out"):
                    i = int(name[10:])
                    if i == 0:
                        pe.wait_ge(sem("sp_ET"), T * (b + 1))
                        take("sp_out_read", T * (b + 1))
                    assert bank["freed"] == "sp_out_read", "the shared bank is taken"
                    for kt in range(T):
                        last = pe.matmul(misc[:, i * P:(i + 1) * P], ET[:, i, kt, :], vsp[:, kt, :],
                                         start=(kt == 0), stop=(kt == T - 1))
                    if i == T - 1:
                        last.then_inc(sem("sp_out"), 1)
                else:
                    assert name == "apply", name

            pe.wait_ge(sem("ident_ready"), 1)
            pe.wait_ge(sem("w_first"), DMA * W_FIRST)
            run(pe, core, piece)

        @block.scalar
        def _(act):
            def evacuate(dst, ready, count, signal):
                act.wait_ge(sem(ready), count)
                act.activation(dst, misc[:, :], ACT.Copy).then_inc(sem(signal), 1)

            def exp_item(r, n):
                g, half_, j = n // (2 * HG), n // HG % 2, n % HG
                if j == 0:
                    if later(2 * G * r + 2 * g + half_ - 1):
                        act.wait_ge(sem("pv_done"), 2 * G * r + 2 * g + half_ - 1)
                act.wait_ge(sem("st_done"), 2 * H * r + n + 1)
                act.activation(pT[half_][:, j, :, :], stb[n % 2][:, :, :], ACT.Exp, scale=SCALE
                               ).then_inc(sem("exp_done"), 1)

            def core(like, r, n, i):
                if like == 0 and n == 0 and i == 0:
                    act.wait_ge(sem("w_in"), DMA * W_DMAS)
                    act.activation(sig[:, 0:1], lam[:, :], ACT.Exp, scale=-1.0).then_inc(sem("lam_exp"), 1)
                if i % 2 and lagging(like, n, LAG):
                    exp_item(r if n >= LAG else r - 1, 2 * ((n - LAG) % H) + i // 2)
                if i == 0 and lagging(like, n, LAG + 2) and (n - LAG - 2) % 4 == 3:
                    m, r_ = (n - LAG - 2) % H, r if n >= LAG + 2 else r - 1
                    act.wait_ge(sem("pv_done"), 2 * (G * r_ + m // 4 + 1))
                    if later(G * r_ + m // 4):
                        act.wait_ge(sem("o_turned"), G * r_ + m // 4)
                    act.activation(oT[:, :], pv[:, :], ACT.Copy).then_inc(sem("oT_done"), 1)

            def piece(name, k, r, b):
                if name == "turn":
                    evacuate(xnT[k][:, :], f"T_{k}", b + 1, f"xnT_{k}")
                elif name in ("project_q", "project_k"):
                    j = int(name == "project_k")
                    act.wait_ge(sem("qk_proj"), 2 * (r + 1) + j + 1)
                    if later(2 * (r + 1)):
                        act.wait_ge(sem("parts"), 2 * (r + 1))
                    if later(DMA * (3 * PARTS - 1) * (r + 1)):
                        act.wait_ge(sem("parts_out"), DMA * (3 * PARTS - 1) * (r + 1))
                    act.activation(qf[:, j, :], misc[:, :], ACT.Identity, bias=colb[k][:, j:j + 1]
                                   ).then_inc(sem("proj_done"), 1)
                    act.activation(split[:, j, 0, :], misc[:, :], ACT.Identity, bias=colb[k][:, j:j + 1]
                                   ).then_inc(sem("proj_done"), 1)
                elif name == "project_v":
                    if later(r + 1):
                        act.wait_ge(sem("v_ready"), r + 1)
                    evacuate(vstage[:, :, :], "v_proj", r + 2, "v_staged")
                elif name == "turn_context":
                    evacuate(ctxT[:, :], f"T_ctx_{k}", b + 1, f"ctxT_{k}")
                elif name == "score":
                    evacuate(srow[:, :], f"score_{k}", b + 1, f"srow_{k}")
                elif name == "own_score":
                    own = misc_t[:, :, 0]
                    act.wait_ge(sem(f"T_own_{k}"), b + 1)
                    act.activation(scol[:, :], own, ACT.Copy).then_inc(sem(f"scol_{k}"), 1)
                    act.activation(gate[:, 0, :], own, ACT.Exp, scale=-1.0).then_inc(sem(f"gate_exp_{k}"), 1)
                elif name.startswith("hidden"):
                    f = int(name[6:])
                    func, bias = (ACT.Relu, col1["L"]) if k == "L1" else (ACT.Identity, col1["F"])
                    act.wait_ge(sem(f"hid_{k}"), FT * b + f + 1)
                    act.activation(hT[:, f, :], hidden_bank(r, f)[:, :], func, bias=bias[:, f:f + 1]).then_inc(sem(f"act_{k}"), 1)
                elif name == "gelu":
                    act.wait_ge(sem(f"act_{k}"), FT * (b + 1))
                    act.activation(hT[:, :, :], hT[:, :, :], ACT.Gelu_apprx_tanh).then_inc(sem(f"gelu_{k}"), 1)
                elif name in ("sparse_q", "sparse_k"):
                    j = int(name == "sparse_k")
                    act.wait_ge(sem("sp_proj"), 2 * b + j + 1)
                    act.activation(qkT[:, j, :], misc[:, :], ACT.Identity, bias=colp[:, j:j + 1]
                                   ).then_inc(sem("sp_qk"), 1)
                elif name == "sparse_score":
                    act.wait_ge(sem("sp_bias"), T * b + k + 1)
                    act.activation(E[:, k, :], misc[:, :], ACT.Exp, bias=smax[:, 1, k:k + 1], scale=R ** -0.5,
                                   accum_out=sall[:, k:k + 1]).then_inc(sem("sp_exp"), 1)
                elif name == "sparse_turn":
                    act.wait_ge(sem("sp_T"), T * b + k + 1)
                    act.activation(ET[:, k, :, :], misc_t, ACT.Copy).then_inc(sem("sp_ET"), 1)

            act.wait_ge(sem("w_first"), DMA * W_FIRST)
            run(act, core, piece)

        @block.vector
        def _(dve):
            def stats_of(k, b):
                if k != "A":
                    ready, unit = X_READY[k]
                    dve.wait_ge(sem(ready), unit * (b + 1))
                    apart(dve, b)
                elif isinstance(b, int) and b == 0:
                    dve.wait_ge(sem("x_first"), DMA)
                else:
                    dve.wait_ge(sem("x_in"), DMA)
                steps = Steps(dve, f"norm_steps_{k}", b, T)
                for i in range(T):
                    steps.did(dve.bn_stats(stats[k][:, i, :], source(k, b, i)))
                steps.wait()
                apart(dve, b)
                for i in range(T):
                    dve.bn_aggr(mv[k][:, i, :], stats[k][:, i, :]).then_inc(sem(f"aggr_{k}"), 1)
                steps.end()

            def affine(k, b, g, be, dst, ready):
                steps = Steps(dve, f"affine_steps_{k}", b, 1)
                dve.wait_ge(sem(f"xn_{k}"), b + 1)
                steps.did(dve.tensor_tensor(dst, xn[k][:, :, :], bc(g), ALU.mult))
                steps.wait()
                steps.end()
                dve.tensor_tensor(dst, dst, bc(be), ALU.add).then_inc(sem(ready), 1)

            def apply(k, b):
                dve.wait_ge(sem(f"rstd_{k}"), b + 1)
                dst = batch(b, base) if k == "B" else xn[k]
                for i in range(T):
                    last = dve.tensor_scalar(dst[:, i, :], source(k, b, i), mv[k][:, i, 0:1], rstd[k][:, i:i + 1],
                                             ALU.subtract, ALU.mult)
                last.then_inc(sem(f"xn_{k}"), 1)
                if k == "L1":
                    affine("L1", b, "g1", "be1", x1n[:, :, :], "x1n_ready")
                if k == "L2":
                    affine("L2", b, "g2", "be2", proj[:, :, :], "y_ready")
                    dve.wait_ge(sem("y_ready"), b + 1)
                    dve.tensor_tensor(batch(b), batch(b), proj[:, :, :], ALU.add).then_inc(sem("x_layer"), 1)

            def max_parts(r, g):
                steps = Steps(dve, "max_steps", G * r + g, 2)
                if later(PARTS * DMA * (r + (g > 0))):
                    dve.wait_ge(sem(f"mrow_in{(g - 1) % G}"), PARTS * DMA * (r + (g > 0)))
                dve.wait_ge(sem("max_T"), G * r + g + 1)
                rows_ = misc[0:HG * T, 0:P]
                steps.did(dve.tensor_copy(msp[:, 0, :], rows_))
                steps.wait()
                dve.tensor_tensor(mres[:, :], rows_, msp[:, 0, :], ALU.subtract).then_inc(sem("max_read"), 1)
                dve.wait_ge(sem("max_read"), G * r + g + 1)
                steps.did(dve.tensor_copy(msp[:, 1, :], mres[:, :]))
                steps.wait()
                steps.end()
                dve.tensor_tensor(msp[:, 2, :], mres[:, :], msp[:, 1, :], ALU.subtract).then_inc(sem("max_parts"), 1)

            turned = misc[:, :].rearrange("p (t j c) -> p t j c", t=T, c=VW)

            def context(r, g):
                dve.wait_ge(sem("o_turned"), G * r + g + 1)
                dve.reciprocal(rden[:, :, :, :], turned[:, :, :, DH:DH + 1]).then_inc(sem("rden"), 1)
                dve.wait_ge(sem("rden"), G * r + g + 1)
                out = ctxt[:, :, g * HG * DH:(g + 1) * HG * DH].rearrange("p t (j d) -> p t j d", d=DH)
                dve.tensor_tensor(out, turned[:, :, :, 0:DH], rden[:, :, :, :].broadcast_to([P, T, HG, DH]),
                                  ALU.mult).then_inc(sem("ctx_done"), 1)

            def core(like, r, n, i):
                if like == 0 and n == 0 and i == 0:
                    rest_of_setup()
                if like < ROUNDS:
                    c, col = n * T + i, n % HG * T + i
                    dve.wait_ge(sem("s_done"), H * T * r + c + 1)
                    dve.tensor_reduce(negm[:, n // HG, col:col + 1], sbank[c % 2][:, :], AX.X, ALU.max,
                                      negate=True).then_inc(sem("max_done"), 1)
                if i == 1 and n % HG == 0 and (n > 0 or like > 0) and (n == 0 or like < ROUNDS):
                    max_parts(*((r, n // HG - 1) if n else (r - 1, G - 1)))
                if i == T - 1 and lagging(like, n, LAG + 2) and (n - LAG - 2) % 4 == 3:
                    context(r if n >= LAG + 2 else r - 1, (n - LAG - 2) % H // 4)

            SPARSE_STEPS = T + 2 * T * (KEEP // 8 + 1) + 4

            def top(b, quarter):
                n, replace, tiles = quarter // 4, quarter % 4 // 2, range(quarter % 2 * 2, quarter % 2 * 2 + 2)
                whole, rest = n < KEEP // 8, KEEP % 8
                after_memset = not whole and quarter % 4 == 3
                steps = Steps(dve, "sparse_steps", b, SPARSE_STEPS, T + 2 * quarter + after_memset)
                from_ = W if n else E
                if quarter == 0:
                    dve.wait_ge(sem("sp_exp"), T * (b + 1))
                steps.wait()
                if not whole and quarter % 4 == 2:
                    steps.did(dve.memset(top8[:, :, rest:8], -1.0))
                    steps.wait()
                for i in tiles:
                    if replace:
                        steps.did(dve.match_replace(W[:, i, :], top8[:, i, :], from_[:, i, :], -1.0))
                    else:
                        steps.did(dve.max(top8[:, i, :], from_[:, i, :]))

            def stacks_at_rest():
                dve.memset(qst[:, :, :], 0.0).then_inc(sem("stack_init"), 1)
                dve.memset(kst[:, :, :], 0.0).then_inc(sem("stack_init"), 1)
                dve.memset(vp[:, :, :, :], 0.0).then_inc(sem("stack_init"), 1)
                dve.memset(zrows[:, :], 0.0).then_inc(sem("stack_init"), 1)
                dve.wait_ge(sem("stack_init"), 4)
                dve.memset(kst[MROW:MROW + PARTS, :, :], 1.0).then_inc(sem("stack_init"), 1)
                dve.memset(vp[:, :, :, DH:DH + 1], 1.0).then_inc(sem("stack_init"), 1)

            def piece(name, k, r, b):
                if name == "stats":
                    stats_of(k, b)
                elif name == "apply":
                    apply(k, b)
                    if isinstance(r, int) and r == -1:
                        stacks_at_rest()
                elif name == "project_out":
                    dve.wait_ge(sem(f"proj_{k}"), b + 1)
                    dve.tensor_tensor(proj[:, :, :], misc_t, bc(f"bo_{k}"), ALU.add).then_inc(sem(f"proj_read_{k}"), 1)
                    dve.wait_ge(sem(f"proj_read_{k}"), b + 1)
                    if k == "A":
                        dve.tensor_tensor(batch(b), batch(b), proj[:, :, :], ALU.add).then_inc(sem("x_attn"), 1)
                    else:
                        dve.wait_ge(sem("sp_out_read"), T * (b + 1))
                        dve.scalar_tensor_tensor(x1[:, :, :], proj[:, :, :], sig[:, 2:3], batch(b, base),
                                                 ALU.mult, ALU.add).then_inc(sem("x1_ready"), 1)
                elif name == "rank":
                    dve.wait_ge(sem(f"gate_exp_{k}"), b + 1)
                    steps = Steps(dve, f"route_steps_{k}", b, T + 2)
                    for i in range(T):
                        steps.did(dve.scalar_tensor_tensor(junk[:, i, :], srow[:, :], scol[:, i:i + 1],
                                                           earlier[:, i, :], ALU.subtract, ALU.is_gt,
                                                           accum_out=rank[:, i:i + 1]))
                    steps.did(dve.tensor_scalar(gate[:, 1, :], gate[:, 0, :], 1.0, None, ALU.add))
                    steps.wait()
                    steps.did(dve.reciprocal(gate[:, 2, :], gate[:, 1, :]))
                    steps.wait()
                    steps.end()
                    dve.scalar_tensor_tensor(gate[:, 3, :], rank[:, :], float(ROUTED), gate[:, 2, :],
                                             ALU.is_lt, ALU.mult).then_inc(sem(f"gate_{k}"), 1)
                elif name == f"ffn_out{T - 1}" and k != "L1":
                    dve.wait_ge(sem(f"ffn_{k}"), b + 1)
                    dve.tensor_tensor(upd[:, :, :], misc_t, bc("b2"), ALU.add).then_inc(sem(f"ffn_read_{k}"), 1)
                elif name == f"ffn_out{T - 1}":
                    dve.wait_ge(sem("ffn_L1"), b + 1)
                    dve.tensor_tensor(y1[:, :, :], misc_t, bc("ff2b"), ALU.add).then_inc(sem("ffn_read_L1"), 1)
                    dve.wait_ge(sem("ffn_read_L1"), b + 1)
                    dve.tensor_tensor(y1[:, :, :], y1[:, :, :], x1n[:, :, :], ALU.add).then_inc(sem("y1_ready"), 1)
                elif name == "update":
                    dve.wait_ge(sem(f"gate_{k}"), b + 1)
                    dve.wait_ge(sem(f"ffn_read_{k}"), b + 1)
                    steps = Steps(dve, f"update_steps_{k}", b, T)
                    for i in range(T):
                        steps.did(dve.scalar_tensor_tensor(upd[:, i, :], upd[:, i, :], gate[:, 3, i:i + 1],
                                                           xn[k][:, i, :], ALU.mult, ALU.add))
                    steps.wait()
                    steps.end()
                    dve.tensor_tensor(batch(b), batch(b), upd[:, :, :], ALU.add).then_inc(sem(X_DONE[k]), 1)
                elif name == "sparse_v":
                    dve.wait_ge(sem("sp_v"), b + 1)
                    dve.tensor_tensor(vsp[:, :, :], misc_t, bc("bvp"), ALU.add).then_inc(sem("sp_v_in"), 1)
                elif name == "sparse_score":
                    steps = Steps(dve, "sparse_steps", b, SPARSE_STEPS, k)
                    dve.wait_ge(sem("sp_score"), T * b + k + 1)
                    steps.did(dve.tensor_reduce(smax[:, 0, k:k + 1], misc[:, :], AX.X, ALU.max))
                    steps.wait()
                    dve.tensor_scalar(smax[:, 1, k:k + 1], smax[:, 0, k:k + 1], -R ** -0.5, None, ALU.mult
                                      ).then_inc(sem("sp_bias"), 1)
                elif name == "top":
                    top(b, k)
                elif name == "sparse_keep":
                    steps = Steps(dve, "sparse_steps", b, SPARSE_STEPS, SPARSE_STEPS - 3)
                    steps.wait()
                    for i in range(T):
                        dve.scalar_tensor_tensor(W[:, i, :], W[:, i, :], 0.0, E[:, i, :], ALU.is_lt, ALU.mult,
                                                 accum_out=ssel[:, i:i + 1]).then_inc(sem("sp_kept"), 1)
                    dve.wait_ge(sem("sp_kept"), T * (b + 1))
                    steps.did(dve.scalar_tensor_tensor(rsp[:, 0, :], sall[:, :], 1e-9, ssel[:, :], ALU.mult, ALU.add))
                    steps.wait()
                    steps.did(dve.reciprocal(rsp[:, 1, :], rsp[:, 0, :]))
                    steps.wait()
                    steps.did(dve.tensor_scalar(rsp[:, 0, :], rsp[:, 1, :], sig[:, 3:4], None, ALU.mult))
                    steps.end()
                elif name == f"sparse_out{T - 1}":
                    dve.wait_ge(sem("sparse_steps"), SPARSE_STEPS * (b + 1))
                    dve.wait_ge(sem("sp_out"), b + 1)
                    for i in range(T):
                        dve.scalar_tensor_tensor(base[:, b * T + i, :], misc_t[:, i, :], rsp[:, 0, i:i + 1],
                                                 base[:, b * T + i, :], ALU.mult, ALU.add
                                                 ).then_inc(sem("sp_out_read"), 1)

            def rest_of_setup():
                dve.wait_ge(sem("w_in"), DMA * W_DMAS)
                dve.wait_ge(sem("earlier_ready"), 1)
                dve.tensor_copy(wr[:, :], wr_col[:, :].broadcast_to([P, P])).then_inc(sem("wr_ready"), 1)
                dve.wait_ge(sem("lam_exp"), 1)
                dve.tensor_scalar(sig[:, 1:2], sig[:, 0:1], 1.0, None, ALU.add).then_inc(sem("sig_steps"), 1)
                dve.wait_ge(sem("sig_steps"), 1)
                dve.reciprocal(sig[:, 2:3], sig[:, 1:2]).then_inc(sem("sig_steps"), 1)
                dve.wait_ge(sem("sig_steps"), 2)
                dve.tensor_scalar(sig[:, 3:4], sig[:, 2:3], -1.0, 1.0, ALU.mult, ALU.add).then_inc(sem("sig_steps"), 1)
                dve.wait_ge(sem("sig_steps"), 3)

            dve.wait_ge(sem("w_first"), DMA * W_FIRST)
            run(dve, core, piece)


def kernel(**inputs):
    import concourse.bacc as bacc
    from concourse.bass_utils import run_bass_kernel_spmd

    a = {k: np.asarray(v) for k, v in inputs.items()}
    m = np.arange(D)

    def circulant(name):
        return a[name][(m[None, :] - m[:, None]) % D]

    A, L = "L0_attn_a_", "L0_attn_b_"
    arrays = {
        "x": a[A + "x"].reshape(B * SEQ, D),
        "w_A": np.stack([circulant(f"{A}w{n}_c") for n in "qkv"], 1),
        "wo_A": circulant(A + "wo_c"),
        "b_A": np.concatenate([a[f"{A}w{n}_b"] for n in "qkv"]),
        "bo_A": a[A + "wo_b"],
        "w_B": a[L + "in_proj_w"].T.reshape(D, 3, D),
        "wo_B": a[L + "out_proj_w"].T,
        "b_B": a[L + "in_proj_b"],
        "bo_B": a[L + "out_proj_b"],
        "QpT": a[L + "Qp_w"].T, "Qpb": a[L + "Qp_b"],
        "KpT": a[L + "Kp_w"].T, "Kpb": a[L + "Kp_b"],
        "VpT": a[L + "Vp_w"].T, "Vpb": a[L + "Vp_b"],
        "lam": a[L + "lam"].reshape(1),
        "ff1T": a[L + "ff1_w"].T, "ff1b": a[L + "ff1_b"].reshape(FT, P).T,
        "ff2T": a[L + "ff2_w"].T, "ff2b": a[L + "ff2_b"],
        "ln1g": a[L + "ln1_g"], "ln1b": a[L + "ln1_b"], "ln2g": a[L + "ln2_g"], "ln2b": a[L + "ln2_b"],
        "wr": a["L0_ffn_w_router"], "W1": a["L0_ffn_W1"], "b1": a["L0_ffn_b1"].reshape(FT, P).T,
        "W2": a["L0_ffn_W2"], "b2": a["L0_ffn_b2"],
    }
    arrays = {k: np.ascontiguousarray(v) for k, v in arrays.items()}
    nc = bacc.Bacc("TRN2", target_bir_lowering=False, num_devices=1)
    t = {k: nc.dram_tensor(f"in_{k}", v.shape, F32, kind="ExternalInput").ap() for k, v in arrays.items()}
    t["out"] = nc.dram_tensor("out", (B * SEQ, D), F32, kind="ExternalOutput").ap()
    build(nc, t)
    r = run_bass_kernel_spmd(nc, [{f"in_{k}": v for k, v in arrays.items()}], core_ids=[0])
    return r.results[0]["out"].reshape(B, SEQ, D)
```

```python
from contextlib import ExitStack

import numpy as np
import concourse.bass as bass
import concourse.mybir as mybir
from concourse.alu_op_type import AluOpType as ALU

ACT = mybir.ActivationFunctionType
AX = mybir.AxisListType
F32 = mybir.dt.float32
BF16 = mybir.dt.bfloat16
ds = bass.ds

P = 128
B, SEQ, D = 4, 512, 128
T = SEQ // P
H, DH = 16, 8
G = 4
HG = H // G
IDLES = 16
PARTS = 3
SLOT = PARTS * DH
MROW = 96
VW = 32
FF = 512
FT = FF // P
R = 64
KEEP = int(SEQ * 0.2)
ROUTED = SEQ // 2
LAG = 6
TINY = -2.0 ** -126
EPS = 1e-5
SCALE = DH ** -0.5
DMA = 16
STACK_DMAS = 7


def build(nc, t):
    with ExitStack() as ctx:
        def sb(name, shape, dt=F32):
            return ctx.enter_context(nc.sbuf_tensor(name, shape, dt))

        def ps(name, shape, dt=F32):
            return ctx.enter_context(nc.psum_tensor(name, shape, dt))

        sems = {}

        def sem(name):
            if name not in sems:
                sems[name] = ctx.enter_context(nc.semaphore(name))
            return sems[name]

        ident = sb("ident", [P, P])
        earlier = sb("earlier", [P, T, SEQ], BF16)
        w = {k: sb(f"w_{k}", [P, 3, P]) for k in "AB"}
        wo = {k: sb(f"wo_{k}", [P, P]) for k in "AB"}
        wr_col = sb("wr_col", [P, 1])
        wr = sb("wr", [P, P])
        w1 = sb("w1", [P, FF])
        w2 = sb("w2", [P, FT, D])
        ff1 = sb("ff1", [P, FF])
        ff2 = sb("ff2", [P, FT, D])
        wqp = sb("wqp", [P, 2, P])
        wvp = sb("wvp", [P, P])
        colb = {k: sb(f"colb_{k}", [P, 2]) for k in "AB"}
        colp = sb("colp", [P, 2])
        col1 = {"F": sb("col_b1", [P, FT]), "L": sb("col_ff1b", [P, FT])}
        rows = {}
        bv = sb("bv", [P, 2, P])
        for name in ("bo_A", "bo_B", "bvp", "b2", "ff2b", "g1", "be1", "g2", "be2"):
            rows[name] = sb(f"row_{name}", [P, P])
        lam = sb("lam", [P, 1])
        sig = sb("sig", [P, 4])
        half = sb("half", [P, T])
        eps = sb("eps", [P, T])
        idle = sb("idle", [1, IDLES])

        x = sb("x", [P, B * T, D])
        LNS = ("A", "F1", "B", "L1", "L2", "F2")
        stats = {k: sb(f"stats_{k}", [P, T, 6]) for k in LNS}
        mv = {k: sb(f"mv_{k}", [P, T, 2]) for k in LNS}
        vare = {k: sb(f"vare_{k}", [P, T]) for k in LNS}
        rstd = {k: sb(f"rstd_{k}", [P, T]) for k in LNS}
        xn = {k: sb(f"xn_{k}", [P, T, D]) for k in LNS if k != "B"}
        xnT = {"A": sb("xnT_att", [P, SEQ]), "F1": sb("xnT_ffn", [P, SEQ])}
        xnT.update(B=xnT["A"], L1=xnT["F1"], F2=xnT["F1"])

        qf = sb("qf", [P, 2, SEQ])
        qr = sb("qr", [P, SEQ])
        split = sb("split", [P, 2, PARTS, SEQ], BF16)
        qst = sb("qst", [P, H, SEQ], BF16)
        kst = sb("kst", [P, H, SEQ], BF16)
        zrows = sb("zrows", [PARTS, SEQ], BF16)
        vstage = sb("vstage", [P, T, D])
        vp = sb("vp", [P, T, H, VW])
        negm = sb("negm", [P, G, HG * T])
        mfull = sb("mfull", [HG * T, P])
        mres = sb("mres", [HG * T, P])
        msp = sb("msp", [HG * T, PARTS, P], BF16)
        pT = [sb(f"pT{n}", [P, HG, 2, SEQ]) for n in range(2)]
        oT = sb("oT", [P, SEQ])
        rden = sb("rden", [P, T, HG, 1])
        ctxt = sb("ctxt", [P, T, D])
        ctxT = sb("ctxT", [P, SEQ])
        proj = sb("proj", [P, T, D])

        srow = sb("srow", [P, SEQ])
        junk = sb("junk", [P, T, SEQ], BF16)
        scol = sb("scol", [P, T])
        rank = sb("rank", [P, T])
        gate = sb("gate", [P, 4, T])
        hT = sb("hT", [P, FT, SEQ])
        upd = sb("upd", [P, T, D])

        qkT = sb("qkT", [P, 2, SEQ])
        vsp = sb("vsp", [P, T, D])
        smax = sb("smax", [P, 2, T])
        E = sb("E", [P, T, SEQ])
        W = sb("W", [P, T, SEQ])
        top8 = sb("top8", [P, T, 8])
        sall = sb("sall", [P, T])
        ssel = sb("ssel", [P, T])
        rsp = sb("rsp", [P, 2, T])
        ET = E[:, :, :].rearrange("p t (k q) -> p t k q", q=P)
        base = sb("base", [P, B * T, D])
        x1 = sb("x1", [P, T, D])
        x1n = sb("x1n", [P, T, D])
        y1 = sb("y1", [P, T, D])

        sbank = [ps(f"sbank{n}", [P, SEQ]) for n in range(3)]
        stb = [ps(f"stb{n}", [P, SEQ]) for n in range(3)]
        pv = ps("pv", [P, SEQ])
        misc = ps("misc", [P, SEQ])
        misc_t = misc[:, :].rearrange("p (t d) -> p t d", t=T)

        qd = nc.dram_tensor("q_parts", (H, PARTS, DH, SEQ), BF16, kind="Internal").ap()
        kd = nc.dram_tensor("k_parts", (H, 2 * PARTS - 1, DH, SEQ), BF16, kind="Internal").ap()
        x_tiles = t["x"].rearrange("(t p) d -> p t d", p=P)
        o_tiles = t["out"].rearrange("(t p) d -> p t d", p=P)

        def later(count):
            return not isinstance(count, int) or count > 0

        class Steps:

            def __init__(self, eng, name, b, n, k=0):
                self.eng, self.name, self.base, self.n, self.k = eng, name, b * n, n, k

            def did(self, ins):
                ins.then_inc(sem(self.name), 1)
                self.k += 1

            def wait(self):
                self.eng.wait_ge(sem(self.name), self.base + self.k)

            def end(self):
                assert self.k == self.n, (self.k, self.n)

        def apart(dve, count):
            if not isinstance(count, int):
                place = idle_at.pop()
                dve.memset(idle[:, place:place + 1], 0.0)

        idle_at = list(range(IDLES))

        block = ctx.enter_context(nc.Block())

        X_READY = {"F1": ("x_attn", 1), "B": ("x_ffn1", 1), "L1": ("x1_ready", 1),
                   "L2": ("y1_ready", 1), "F2": ("x_layer", 1)}
        X_DONE = {"F1": "x_ffn1", "F2": "x_ffn2"}

        def batch(b, of=x):
            return of[:, b * T:(b + 1) * T, :] if isinstance(b, int) else of[:, ds(b * T, T), :]

        def source(k, b, i):
            if k == "L1":
                return x1[:, i, :]
            if k == "L2":
                return y1[:, i, :]
            return x[:, b * T + i, :] if isinstance(b, int) else x[:, ds(b * T + i, 1), :]

        def bc(row):
            return rows[row][:, :].unsqueeze(1).broadcast_to([P, T, D])

        def kind(r):
            return ("A", 0) if r < B else ("B", B)

        def prelude(k, first):
            return [(0, "stats", k, first), (2, "apply", k, first), (5, "turn", k, first),
                    (7, "project_q", k, first), (9, "project_k", k, first), (35, "project_v", k, first)]

        def sparse(first):
            out = [(11, "sparse_q", "B", first), (12, "sparse_k", "B", first), (23, "sparse_v", "B", first)]
            at = 26
            for h in range(2):
                tiles = (2 * h, 2 * h + 1)
                out += [((at - 2 + n, 37 + 2 * n)[h], "sparse_score", i, first) for n, i in enumerate(tiles)]
                out += [(at + n, "top", (h, n), first) for n in range(TOP_PIECES)]
                at += TOP_PIECES
                out += [(at, "sparse_keep", h, first)]
                out += [(at + 2 - h + n, "sparse_turn", i, first) for n, i in enumerate(tiles)]
                out += [(at + 4 + n, f"sparse_out{i}", "B", first) for n, i in enumerate(tiles)]
            return out

        def out_projection(k, first, at):
            return [(at, "turn_context", k, first), (at + 2, "project_out", k, first)]

        def norm_turned(k, first, at):
            return [(at, "stats", k, first), (at + 2, "apply", k, first), (at + 5, "turn", k, first)]

        def hidden(k, first, at, spacing, out):
            gelu = [] if k == "L1" else [(at + spacing * (FT - 1), "gelu", k, first)]
            return ([(at + spacing * f, f"hidden{f}", k, first) for f in range(FT)] + gelu
                    + [(out + i, f"ffn_out{i}", k, first) for i in range(T)])

        def ffn(k, first, at, spacing, out):
            return (norm_turned(k, first, at) + [(at + 7, "score", k, first)] + hidden(k, first, at + 8, spacing, out)
                    + [(at + 9, "own_score", k, first), (at + 11, "rank", k, first), (out + T, "update", k, first)])

        def layer_ffn(first, at, out):
            return (norm_turned("L1", first, at) + hidden("L1", first, at + 7, 1, out)
                    + [(out + T + 1, "stats", "L2", first), (out + T + 3, "apply", "L2", first)])

        TOP_PIECES = 2 * (KEEP // 8 + 1)
        STEPS = H * T
        ROUNDS = 2 * B

        def sides(r):
            out = []
            if r + 1 < ROUNDS:
                k, first = kind(r + 1)
                out += prelude(k, first - 1)
                if k == "B":
                    out += [piece for piece in sparse(first - 1) if piece[0] < STEPS]
            if B <= r < ROUNDS:
                out += [(step - STEPS, name, arg, behind) for step, name, arg, behind in sparse(B)
                        if step >= STEPS]
            if 0 < r < ROUNDS:
                k, first = kind(r - 1)
                out += out_projection(k, first + 1, 32)
                out += layer_ffn(first + 1, 36, 50) if k == "B" else ffn("F1", first + 1, 36, 2, 58)
            if B + 2 <= r < ROUNDS:
                out += ffn("F2", B + 2, 5, 1, 27)
            if r < ROUNDS:
                out += [(28, "place_v", r, 0)]
            if r == ROUNDS:
                out += ffn("F2", B + 2, 1, 2, 24) + out_projection("B", B + 1, 32) + layer_ffn(B + 1, 36, 49)
                out += ffn("F2", B + 1, 64, 2, 90)
            by_step = {}
            for piece in sorted(out, key=lambda x: x[0]):
                by_step.setdefault(min(piece[0], STEPS - 2) if r < ROUNDS else piece[0], []).append(piece[1:])
            return by_step

        def lagging(like, n, lag):
            return like > 0 and n < lag or like < ROUNDS and n >= lag

        def group_of_max(like, r, n, i):
            if i == 1 and n % HG == 0 and (n > 0 or like > 0) and (n == 0 or like < ROUNDS):
                return (r, n // HG - 1) if n else (r - 1, G - 1)
            return None

        def st_place(n):
            return n // (HG * T), n // (HG * 2) % 2, n // 2 % HG, n % 2

        def bank_uses(r, n):
            return H * T * r + (n - 2 if n else 0)

        def last_period(r):
            return isinstance(r, int) and r == ROUNDS

        def after_norm(eng, k, b):
            g, be, dst, ready = {"L1": ("g1", "be1", x1n, "x1n_ready"), "L2": ("g2", "be2", proj, "y_ready")}[k]
            eng.wait_ge(sem(f"xn_{k}"), b + 1)
            eng.tensor_tensor(dst[:, :, :], xn[k][:, :, :], bc(g), ALU.mult).then_inc(sem(f"scaled_{k}"), 1)
            eng.wait_ge(sem(f"scaled_{k}"), b + 1)
            eng.tensor_tensor(dst[:, :, :], dst[:, :, :], bc(be), ALU.add).then_inc(sem(ready), 1)
            if k == "L2":
                eng.wait_ge(sem("y_ready"), b + 1)
                eng.tensor_tensor(batch(b), batch(b), proj[:, :, :], ALU.add).then_inc(sem("x_layer"), 1)

        def hidden_bank(r, f):
            return sbank[f % 2] if last_period(r) else misc

        def run(eng, core, piece):
            def period(like, r):
                by_step = sides(like)
                for step in range(max(STEPS, max(by_step) + 1)):
                    n, i = divmod(step, T)
                    if step < STEPS:
                        core(like, r, n, i)
                    for name, arg, behind in by_step.get(step, ()):
                        piece(name, arg, r, r - behind)

            for _, name, arg, _ in prelude("A", 0):
                piece(name, arg, -1, 0)
            period(0, 0)
            with eng.Fori(1, B - 1) as r:
                period(1, r)
            for r in range(B - 1, ROUNDS + 1):
                period(r, r)

        @block.sync
        def _(sp):
            def load(dst, src, name):
                sp.dma_start(dst, src).then_inc(sem(name), DMA)

            load(x[:, 0:T, :], x_tiles[:, 0:T, :], "x_first")
            for k in "AB":
                name = "w_first" if k == "A" else "w_in"
                load(w[k][:, :, :], t[f"w_{k}"], name)
                for j in range(2):
                    load(colb[k][:, j:j + 1], t[f"b_{k}"][j * D:(j + 1) * D].unsqueeze(1), name)
                load(bv[:, int(k == "B"), :], t[f"b_{k}"][2 * D:3 * D].partition_broadcast(P), name)
                if k == "A":
                    load(x[:, T:B * T, :], x_tiles[:, T:B * T, :], "x_in")
                load(wo[k][:, :], t[f"wo_{k}"], "w_in")
                load(rows[f"bo_{k}"][:, :], t[f"bo_{k}"].partition_broadcast(P), "w_in")
            load(wr_col[:, :], t["wr"].unsqueeze(1), "w_in")
            load(w1[:, :], t["W1"], "w_in")
            load(w2[:, :, :], t["W2"].rearrange("(f p) d -> p f d", p=P), "w_in")
            load(ff1[:, :], t["ff1T"], "w_in")
            load(ff2[:, :, :], t["ff2T"].rearrange("(f p) d -> p f d", p=P), "w_in")
            sp.wait_ge(sem("zeros"), 2)
            for j, k in enumerate("QK"):
                load(wqp[:, j, 0:R], t[f"{k}pT"], "w_in")
                load(colp[0:R, j:j + 1], t[f"{k}pb"].unsqueeze(1), "w_in")
            load(wvp[:, :], t["VpT"], "w_in")
            load(col1["F"][:, :], t["b1"], "w_in")
            load(col1["L"][:, :], t["ff1b"], "w_in")
            for row, name in (("bvp", "Vpb"), ("b2", "b2"), ("ff2b", "ff2b"), ("g1", "ln1g"), ("be1", "ln1b"),
                              ("g2", "ln2g"), ("be2", "ln2b")):
                load(rows[row][:, :], t[name].partition_broadcast(P), "w_in")
            load(lam[:, :], t["lam"].partition_broadcast(P), "w_in")

            def value(v):
                return v if isinstance(v, int) else sp.snap(v)

            def store_parts(at, r):
                sp.wait_ge(sem("parts"), at["q_split"])
                for g in range(G):
                    if later(at["restacked"]):
                        sp.wait_ge(sem(f"stack_in{g}"), at["restacked"])
                for s in range(PARTS):
                    sp.dma_start(qd[:, s, :, :], split[:, 0, s, :]).then_inc(sem("parts_out"), DMA)
                sp.wait_ge(sem("parts"), at["k_split"])
                for s in range(2 * PARTS - 1):
                    sp.dma_start(kd[:, s, :, :], split[:, 1, s % PARTS, :]).then_inc(sem("parts_out"), DMA)
                sp.wait_ge(sem("parts_out"), at["stored"])

            def fill_stacks(g, st_over):
                heads = slice(g * HG, (g + 1) * HG)
                if later(st_over):
                    sp.wait_ge(sem("st_done"), st_over)
                done = sem(f"stack_in{g}")
                for n, first in enumerate((0, 2, 1)):
                    lines = slice(n * SLOT, (n + 1) * SLOT)
                    sp.dma_start(qst[lines, heads, :], qd[heads, :, :, :].rearrange("h s d t -> (s d) h t")
                                 ).then_inc(done, DMA)
                    sp.dma_start(kst[lines, heads, :],
                                 kd[heads, first:first + PARTS, :, :].rearrange("h s d t -> (s d) h t")
                                 ).then_inc(done, DMA)
                sp.dma_start(qst[MROW:MROW + PARTS, heads, :],
                             zrows[:, :].unsqueeze(1).broadcast_to([PARTS, HG, SEQ])).then_inc(done, DMA)

            def fill_max(g, split_):
                sp.wait_ge(sem("max_parts"), split_)
                for s in range(PARTS):
                    sp.dma_start(qst[MROW + s:MROW + s + 1, g * HG:(g + 1) * HG, :], msp[:, s, :]
                                 ).then_inc(sem(f"mrow_in{g}"), DMA)

            def store_x(b):
                sp.wait_ge(sem("x_ffn2"), b + 1)
                sp.dma_start(o_tiles[:, b * T:(b + 1) * T, :], batch(b)).then_inc(sem("out"), DMA)

            def next_parts(r):
                return {"q_split": value(2 * r + 1), "k_split": value(2 * r + 2), "restacked": value(STACK_DMAS * r * DMA),
                        "stored": value(DMA * (3 * PARTS - 1) * (r + 1))}

            def group_values(r):
                over = [value(r * H * T + T * HG * (g + 1) - H * T) for g in range(G)]
                return over, [value(G * r + g + 1) for g in range(G)]

            def period(like, r):
                over, parts = group_values(r)
                if like > 0:
                    fill_max(G - 1, value(G * r))
                if like < ROUNDS:
                    fill_stacks(2, over[2])
                    fill_max(0, parts[0])
                    fill_stacks(3, over[3])
                    fill_max(1, parts[1])
                    if like + 1 < ROUNDS:
                        store_parts(next_parts(r + 1), r + 1)
                        over, _ = group_values(r + 1)
                        fill_stacks(0, over[0])
                        fill_max(2, parts[2])
                        fill_stacks(1, over[1])
                    else:
                        fill_max(2, parts[2])
                if like > B + 1:
                    store_x(like - B - 2)

            store_parts(next_parts(0), 0)
            sp.wait_ge(sem("stack_init"), 6)
            fill_stacks(0, 0)
            fill_stacks(1, 0)
            period(0, 0)
            with sp.Fori(1, B - 1) as r:
                period(1, r)
            for r in range(B - 1, ROUNDS + 1):
                period(r, r)
            store_x(B - 1)
            sp.wait_ge(sem("out"), DMA * B)

        W_FIRST = 4
        W_DMAS = 2 * 6 - W_FIRST + 5 + 4 + 3 + 7 + 1

        @block.gpsimd
        def _(pool):
            pool.memset(half[:, :], -0.5).then_inc(sem("pool_init"), 1)
            pool.memset(eps[:, :], EPS).then_inc(sem("pool_init"), 1)
            pool.memset(ident[:, :], 0.0).then_inc(sem("pool_init"), 1)
            pool.wait_ge(sem("pool_init"), 3)
            pool.affine_select(out=ident[:, :], in_=ident[:, :], compare_op=ALU.not_equal, fill=1.0, base=0,
                               pattern=[[-1, P]], channel_multiplier=1).then_inc(sem("ident_ready"), 1)

            def rest_of_setup():
                pool.memset(earlier[:, :, :], TINY).then_inc(sem("pool_init"), 1)
                pool.wait_ge(sem("pool_init"), 4)
                pool.affine_select(out=earlier[:, :, :], in_=earlier[:, :, :], compare_op=ALU.is_gt, fill=0.0, base=0,
                                   pattern=[[P, T], [-1, SEQ]], channel_multiplier=1
                                   ).then_inc(sem("earlier_ready"), 1)

            def rstds(k, b):
                pool.wait_ge(sem(f"aggr_{k}"), T * (b + 1))
                pool.tensor_tensor(vare[k][:, :], mv[k][:, :, 1], eps[:, :], ALU.add).then_inc(sem(f"vare_{k}"), 1)
                pool.wait_ge(sem(f"vare_{k}"), b + 1)
                pool.tensor_tensor(rstd[k][:, :], vare[k][:, :], half[:, :], ALU.pow).then_inc(sem(f"rstd_{k}"), 1)

            def parts(r, j):
                steps = Steps(pool, "split_steps", 2 * r + j, 2)
                if later(2 * r + j):
                    pool.wait_ge(sem("parts"), 2 * r + j)
                pool.wait_ge(sem("proj_done"), 2 * (2 * r + j) + 2)
                if later(DMA * (3 * PARTS - 1) * r):
                    pool.wait_ge(sem("parts_out"), DMA * (3 * PARTS - 1) * r)
                steps.did(pool.tensor_tensor(qr[:, :], qf[:, j, :], split[:, j, 0, :], ALU.subtract))
                steps.did(pool.tensor_tensor(split[:, j, 1, :], qf[:, j, :], split[:, j, 0, :], ALU.subtract))
                steps.wait()
                steps.end()
                pool.tensor_tensor(split[:, j, 2, :], qr[:, :], split[:, j, 1, :], ALU.subtract
                                   ).then_inc(sem("parts"), 1)

            def place_v(like, r):
                bias = bv[:, ds(int(like >= B), 1), :].broadcast_to([P, T, D])
                pool.wait_ge(sem("v_staged"), r + 1)
                if isinstance(r, int) and r == 0:
                    pool.wait_ge(sem("stack_init"), 6)
                if later(2 * G * r):
                    pool.wait_ge(sem("pv_done"), 2 * G * r)
                pool.tensor_tensor(vp[:, :, :, 0:DH], vstage[:, :, :].rearrange("p t (h d) -> p t h d", h=H),
                                   bias.rearrange("p t (h d) -> p t h d", h=H), ALU.add
                                   ).then_inc(sem("v_ready"), 1)

            def max_parts(r, g):
                steps = Steps(pool, "max_steps", G * r + g, 2)
                if later(G * r + g):
                    pool.wait_ge(sem("max_parts"), G * r + g)
                pool.wait_ge(sem("max_read"), 2 * (G * r + g + 1))
                steps.did(pool.tensor_tensor(mres[:, :], mfull[:, :], msp[:, 0, :], ALU.subtract))
                steps.did(pool.tensor_tensor(msp[:, 1, :], mfull[:, :], msp[:, 0, :], ALU.subtract))
                steps.wait()
                steps.end()
                pool.tensor_tensor(msp[:, 2, :], mres[:, :], msp[:, 1, :], ALU.subtract).then_inc(sem("max_parts"), 1)

            def core(like, r, n, i):
                if group_of_max(like, r, n, i):
                    max_parts(*group_of_max(like, r, n, i))

            def piece(name, arg, r, b):
                if name == "stats":
                    rstds(arg, b)
                elif name == "apply" and arg in ("L1", "L2") and not last_period(r):
                    after_norm(pool, arg, b)
                elif name == "project_q":
                    parts(r + 1, 0)
                elif name == "project_k":
                    parts(r + 1, 1)
                    if isinstance(r, int) and r == -1:
                        rest_of_setup()
                elif name == "place_v":
                    place_v(arg, r)

            pool.memset(wqp[:, :, :], 0.0).then_inc(sem("zeros"), 1)
            pool.memset(colp[:, :], 0.0).then_inc(sem("zeros"), 1)
            pool.wait_ge(sem("w_first"), DMA * W_FIRST)
            run(pool, core, piece)

        @block.tensor
        def _(pe):
            bank = {"freed": None, "count": 0}

            def take(freed, count):
                if bank["freed"]:
                    pe.wait_ge(sem(bank["freed"]), bank["count"])
                bank.update(freed=freed, count=count)

            def turn(src, ready, count, signal, freed, freed_count):
                pe.wait_ge(sem(ready), count)
                take(freed, freed_count)
                for i in range(T):
                    last = pe.transpose(misc[:, i * P:(i + 1) * P], src[:, i, :], ident[:, :])
                last.then_inc(sem(signal), 1)

            def token_product(lhsT, rhs, signal, freed, count):
                take(freed, count)
                for i in range(T):
                    last = pe.matmul(misc[:, i * P:(i + 1) * P], lhsT[:, i * P:(i + 1) * P], rhs,
                                     start=True, stop=True)
                last.then_inc(sem(signal), 1)

            def s_tile(r, h, i):
                n = h * T + i
                if i == 0 and h % HG == 0:
                    pe.wait_ge(sem(f"stack_in{h // HG}"), STACK_DMAS * DMA * (r + 1))
                if later(bank_uses(r, n)):
                    pe.wait_ge(sem("max_done"), bank_uses(r, n))
                pe.matmul(sbank[n % 3][:, :], qst[:, h, i * P:(i + 1) * P], kst[:, h, :],
                          start=True, stop=True).then_inc(sem("s_done"), 1)

            def st_item(r, n):
                g, half_, j, c = st_place(n)
                h, kt = g * HG + j, 2 * half_ + c
                if n % (HG * T) == 0:
                    pe.wait_ge(sem(f"mrow_in{g}"), PARTS * DMA * (r + 1))
                if later(bank_uses(r, n)):
                    pe.wait_ge(sem("exp_done"), bank_uses(r, n))
                pe.matmul(stb[n % 3][:, :], kst[:, h, kt * P:(kt + 1) * P], qst[:, h, :],
                          start=True, stop=True).then_inc(sem("st_done"), 1)

            def max_rows(r, g):
                pe.wait_ge(sem("max_done"), H * T * r + (g + 1) * HG * T)
                take("max_read", 2 * (G * r + g + 1))
                pe.transpose(misc[0:HG * T, 0:P], negm[:, g, :], ident[:, :]).then_inc(sem("max_T"), 1)

            def o_quarter(r, g, half_, c):
                if g == 0 and half_ == 0 and c == 0:
                    pe.wait_ge(sem("v_ready"), r + 1)
                pe.wait_ge(sem("exp_done"), H * T * r + HG * (T * g + 2 * (half_ + 1)))
                if half_ == 0 and c == 0:
                    if later(G * r + g):
                        pe.wait_ge(sem("oT_done"), G * r + g)
                for j in range(HG):
                    last = pe.matmul(pv[VW * j:VW * (j + 1), :], vp[:, 2 * half_ + c, HG * g + j, :],
                                     pT[half_][:, j, c, :], start=(2 * half_ + c == 0),
                                     stop=(2 * half_ + c == T - 1))
                if c:
                    last.then_inc(sem("pv_done"), 1)

            def o_turn(r, g):
                pe.wait_ge(sem("oT_done"), G * r + g + 1)
                take("ctx_done", G * r + g + 1)
                for i in range(T):
                    last = pe.transpose(misc[:, i * P:(i + 1) * P], oT[:, i * P:(i + 1) * P], ident[:, :])
                last.then_inc(sem("o_turned"), 1)

            def core(like, r, n, i):
                if n == 0 and i == 0 and like > 0:
                    bank.update(freed="ctx_done", count=G * (r - 1) + 2)
                if n == 0 and i == 0 and like == 0:
                    pe.wait_ge(sem("stack_init"), 6)
                    pe.wait_ge(sem("w_in"), DMA * W_DMAS)
                    pe.wait_ge(sem("wr_ready"), 1)
                if like < ROUNDS:
                    s_tile(r, n, i)
                if group_of_max(like, r, n, i):
                    max_rows(*group_of_max(like, r, n, i))
                if lagging(like, n, LAG):
                    st_item(r if n >= LAG else r - 1, T * ((n - LAG) % H) + i)
                if lagging(like, n, LAG + 2):
                    m, r_ = (n - LAG - 2) % H, r if n >= LAG + 2 else r - 1
                    if (m % 2, i) in ((0, 2), (1, 0)):
                        o_quarter(r_, m // 4, m // 2 % 2, m % 2)
                    if (m % 4, i) == (3, T - 1):
                        o_turn(r_, m // 4)

            def piece(name, k, r, b):
                if name in ("stats", "update", "rank", "place_v", "gelu", "top", "sparse_keep"):
                    return
                if name == "turn":
                    ready = "x1n_ready" if k == "L1" else f"xn_{k}"
                    src = x1n if k == "L1" else batch(b, base) if k == "B" else xn[k]
                    turn(src, ready, b + 1, f"T_{k}", f"xnT_{k}", b + 1)
                elif name in ("project_q", "project_k"):
                    j = int(name == "project_k")
                    pe.wait_ge(sem(f"xnT_{k}"), b + 1)
                    take("proj_done", 2 * (2 * (r + 1) + j) + 2)
                    pe.matmul(misc[:, :], w[k][:, j, :], xnT[k][:, :], start=True, stop=True
                              ).then_inc(sem("qk_proj"), 1)
                elif name == "project_v":
                    token_product(xnT[k], w[k][:, 2, :], "v_proj", "v_staged", r + 2)
                elif name == "turn_context":
                    turn(ctxt, "ctx_done", G * r, f"T_ctx_{k}", f"ctxT_{k}", b + 1)
                elif name == "project_out":
                    pe.wait_ge(sem(f"ctxT_{k}"), b + 1)
                    token_product(ctxT, wo[k][:, :], f"proj_{k}", f"proj_read_{k}", b + 1)
                elif name == "score":
                    pe.wait_ge(sem(f"xnT_{k}"), b + 1)
                    take(f"srow_{k}", b + 1)
                    pe.matmul(misc[:, :], wr[:, :], xnT[k][:, :], start=True, stop=True
                              ).then_inc(sem(f"score_{k}"), 1)
                elif name == "own_score":
                    turn(srow[:, :].rearrange("p (t q) -> p t q", t=T), f"srow_{k}", b + 1, f"T_own_{k}",
                         f"gate_exp_{k}", b + 1)
                elif name.startswith("hidden"):
                    f = int(name[6:])
                    pe.wait_ge(sem(f"xnT_{k}"), b + 1)
                    bank_ = hidden_bank(r, f)
                    if bank_ is misc:
                        take(f"act_{k}", FT * b + f + 1)
                    elif f < 2:
                        pe.wait_ge(sem("max_done"), H * T * ROUNDS)
                    else:
                        pe.wait_ge(sem(f"act_{k}"), FT * b + f - 1)
                    w_in = ff1 if k == "L1" else w1
                    pe.matmul(bank_[:, :], w_in[:, f * P:(f + 1) * P], xnT[k][:, :], start=True, stop=True
                              ).then_inc(sem(f"hid_{k}"), 1)
                elif name.startswith("ffn_out"):
                    i = int(name[7:])
                    if i == 0:
                        pe.wait_ge(sem(f"act_{k}"), FT * (b + 1))
                        if k != "L1":
                            pe.wait_ge(sem(f"gelu_{k}"), b + 1)
                        take(f"ffn_read_{k}", b + 1)
                    assert bank["freed"] == f"ffn_read_{k}", "the shared bank is taken"
                    w_out = ff2 if k == "L1" else w2
                    for f in range(FT):
                        last = pe.matmul(misc[:, i * P:(i + 1) * P], hT[:, f, i * P:(i + 1) * P],
                                         w_out[:, f, :], start=(f == 0), stop=(f == FT - 1))
                    if i == T - 1:
                        last.then_inc(sem(f"ffn_{k}"), 1)
                elif name in ("sparse_q", "sparse_k"):
                    j = int(name == "sparse_k")
                    take("sp_qk", 2 * b + j + 1)
                    pe.matmul(misc[:, :], wqp[:, j, :], xnT["B"][:, :], start=True, stop=True
                              ).then_inc(sem("sp_proj"), 1)
                elif name == "sparse_v":
                    token_product(xnT["B"], wvp[:, :], "sp_v", "sp_v_in", b + 1)
                elif name == "sparse_score":
                    pe.wait_ge(sem("sp_qk"), 2 * (b + 1))
                    take("sp_exp", T * b + k + 1)
                    pe.matmul(misc[:, :], qkT[:, 0, k * P:(k + 1) * P], qkT[:, 1, :], start=True, stop=True
                              ).then_inc(sem("sp_score"), 1)
                elif name == "sparse_turn":
                    pe.wait_ge(sem("sp_kept"), T * b + k + 1)
                    take("sp_ET", T * b + k + 1)
                    for kt in range(T):
                        last = pe.transpose(misc[:, kt * P:(kt + 1) * P], W[:, k, kt * P:(kt + 1) * P], ident[:, :])
                    last.then_inc(sem("sp_T"), 1)
                elif name.startswith("sparse_out"):
                    i = int(name[10:])
                    if i % 2 == 0:
                        pe.wait_ge(sem("sp_ET"), T * b + i + 2)
                        take("sp_out_read", T * b + i + 2)
                    assert bank["freed"] == "sp_out_read", "the shared bank is taken"
                    for kt in range(T):
                        last = pe.matmul(misc[:, i * P:(i + 1) * P], ET[:, i, kt, :], vsp[:, kt, :],
                                         start=(kt == 0), stop=(kt == T - 1))
                    if i % 2:
                        last.then_inc(sem("sp_out"), 1)
                else:
                    assert name == "apply", name

            pe.wait_ge(sem("ident_ready"), 1)
            pe.wait_ge(sem("w_first"), DMA * W_FIRST)
            run(pe, core, piece)

        @block.scalar
        def _(act):
            def evacuate(dst, ready, count, signal):
                act.wait_ge(sem(ready), count)
                act.activation(dst, misc[:, :], ACT.Copy).then_inc(sem(signal), 1)

            def max_out(r, g):
                if later(G * r + g):
                    act.wait_ge(sem(f"mrow_in{(g - 1) % G}"), PARTS * DMA * (r + (g > 0)))
                act.wait_ge(sem("max_T"), G * r + g + 1)
                act.activation(mfull[:, :], misc[0:HG * T, 0:P], ACT.Copy).then_inc(sem("max_read"), 1)
                act.activation(msp[:, 0, :], misc[0:HG * T, 0:P], ACT.Copy).then_inc(sem("max_read"), 1)

            def exp_item(r, n):
                g, half_, j, c = st_place(n)
                if j == 0 and c == 0:
                    if later(2 * G * r + 2 * g + half_ - 1):
                        act.wait_ge(sem("pv_done"), 2 * G * r + 2 * g + half_ - 1)
                act.wait_ge(sem("st_done"), H * T * r + n + 1)
                act.activation(pT[half_][:, j, c, :], stb[n % 3][:, :], ACT.Exp, scale=SCALE
                               ).then_inc(sem("exp_done"), 1)

            def core(like, r, n, i):
                if like == 0 and n == 0 and i == 0:
                    act.wait_ge(sem("w_in"), DMA * W_DMAS)
                    act.activation(sig[:, 0:1], lam[:, :], ACT.Exp, scale=-1.0).then_inc(sem("lam_exp"), 1)
                if group_of_max(like, r, n, i):
                    max_out(*group_of_max(like, r, n, i))
                if lagging(like, n, LAG):
                    exp_item(r if n >= LAG else r - 1, T * ((n - LAG) % H) + i)
                if i == 0 and lagging(like, n, LAG + 2) and (n - LAG - 2) % 4 == 3:
                    m, r_ = (n - LAG - 2) % H, r if n >= LAG + 2 else r - 1
                    act.wait_ge(sem("pv_done"), 2 * (G * r_ + m // 4 + 1))
                    if later(G * r_ + m // 4):
                        act.wait_ge(sem("o_turned"), G * r_ + m // 4)
                    act.activation(oT[:, :], pv[:, :], ACT.Copy).then_inc(sem("oT_done"), 1)

            def piece(name, k, r, b):
                if name == "turn":
                    evacuate(xnT[k][:, :], f"T_{k}", b + 1, f"xnT_{k}")
                elif name in ("project_q", "project_k"):
                    j = int(name == "project_k")
                    act.wait_ge(sem("qk_proj"), 2 * (r + 1) + j + 1)
                    if later(2 * (r + 1)):
                        act.wait_ge(sem("parts"), 2 * (r + 1))
                    if later(DMA * (3 * PARTS - 1) * (r + 1)):
                        act.wait_ge(sem("parts_out"), DMA * (3 * PARTS - 1) * (r + 1))
                    act.activation(qf[:, j, :], misc[:, :], ACT.Identity, bias=colb[k][:, j:j + 1]
                                   ).then_inc(sem("proj_done"), 1)
                    act.activation(split[:, j, 0, :], misc[:, :], ACT.Identity, bias=colb[k][:, j:j + 1]
                                   ).then_inc(sem("proj_done"), 1)
                elif name == "project_v":
                    if later(r + 1):
                        act.wait_ge(sem("v_ready"), r + 1)
                    evacuate(vstage[:, :, :], "v_proj", r + 2, "v_staged")
                elif name == "turn_context":
                    evacuate(ctxT[:, :], f"T_ctx_{k}", b + 1, f"ctxT_{k}")
                elif name == "score":
                    evacuate(srow[:, :], f"score_{k}", b + 1, f"srow_{k}")
                elif name == "own_score":
                    own = misc_t[:, :, 0]
                    act.wait_ge(sem(f"T_own_{k}"), b + 1)
                    act.activation(scol[:, :], own, ACT.Copy).then_inc(sem(f"scol_{k}"), 1)
                    act.activation(gate[:, 0, :], own, ACT.Exp, scale=-1.0).then_inc(sem(f"gate_exp_{k}"), 1)
                elif name.startswith("hidden"):
                    f = int(name[6:])
                    func, bias = (ACT.Relu, col1["L"]) if k == "L1" else (ACT.Identity, col1["F"])
                    act.wait_ge(sem(f"hid_{k}"), FT * b + f + 1)
                    act.activation(hT[:, f, :], hidden_bank(r, f)[:, :], func, bias=bias[:, f:f + 1]).then_inc(sem(f"act_{k}"), 1)
                elif name == "gelu":
                    act.wait_ge(sem(f"act_{k}"), FT * (b + 1))
                    act.activation(hT[:, :, :], hT[:, :, :], ACT.Gelu_apprx_tanh).then_inc(sem(f"gelu_{k}"), 1)
                elif name in ("sparse_q", "sparse_k"):
                    j = int(name == "sparse_k")
                    act.wait_ge(sem("sp_proj"), 2 * b + j + 1)
                    act.activation(qkT[:, j, :], misc[:, :], ACT.Identity, bias=colp[:, j:j + 1]
                                   ).then_inc(sem("sp_qk"), 1)
                elif name == "sparse_score":
                    act.wait_ge(sem("sp_bias"), T * b + k + 1)
                    act.activation(E[:, k, :], misc[:, :], ACT.Exp, bias=smax[:, 1, k:k + 1], scale=R ** -0.5,
                                   accum_out=sall[:, k:k + 1]).then_inc(sem("sp_exp"), 1)
                elif name == "sparse_turn":
                    act.wait_ge(sem("sp_T"), T * b + k + 1)
                    act.activation(ET[:, k, :, :], misc_t, ACT.Copy).then_inc(sem("sp_ET"), 1)

            act.wait_ge(sem("w_first"), DMA * W_FIRST)
            run(act, core, piece)

        @block.vector
        def _(dve):
            def stats_of(k, b):
                if k != "A":
                    ready, unit = X_READY[k]
                    dve.wait_ge(sem(ready), unit * (b + 1))
                    apart(dve, b)
                elif isinstance(b, int) and b == 0:
                    dve.wait_ge(sem("x_first"), DMA)
                else:
                    dve.wait_ge(sem("x_in"), DMA)
                steps = Steps(dve, f"norm_steps_{k}", b, T)
                for i in range(T):
                    steps.did(dve.bn_stats(stats[k][:, i, :], source(k, b, i)))
                steps.wait()
                apart(dve, b)
                for i in range(T):
                    dve.bn_aggr(mv[k][:, i, :], stats[k][:, i, :]).then_inc(sem(f"aggr_{k}"), 1)
                steps.end()

            def apply(k, b):
                dve.wait_ge(sem(f"rstd_{k}"), b + 1)
                dst = batch(b, base) if k == "B" else xn[k]
                for i in range(T):
                    last = dve.tensor_scalar(dst[:, i, :], source(k, b, i), mv[k][:, i, 0:1], rstd[k][:, i:i + 1],
                                             ALU.subtract, ALU.mult)
                last.then_inc(sem(f"xn_{k}"), 1)

            turned = misc[:, :].rearrange("p (t j c) -> p t j c", t=T, c=VW)

            def context(r, g):
                dve.wait_ge(sem("o_turned"), G * r + g + 1)
                dve.reciprocal(rden[:, :, :, :], turned[:, :, :, DH:DH + 1]).then_inc(sem("rden"), 1)
                dve.wait_ge(sem("rden"), G * r + g + 1)
                out = ctxt[:, :, g * HG * DH:(g + 1) * HG * DH].rearrange("p t (j d) -> p t j d", d=DH)
                dve.tensor_tensor(out, turned[:, :, :, 0:DH], rden[:, :, :, :].broadcast_to([P, T, HG, DH]),
                                  ALU.mult).then_inc(sem("ctx_done"), 1)

            def core(like, r, n, i):
                if like == 0 and n == 0 and i == 0:
                    rest_of_setup()
                if like < ROUNDS:
                    c, col = n * T + i, n % HG * T + i
                    dve.wait_ge(sem("s_done"), H * T * r + c + 1)
                    dve.tensor_reduce(negm[:, n // HG, col:col + 1], sbank[c % 3][:, :], AX.X, ALU.max,
                                      negate=True).then_inc(sem("max_done"), 1)
                if i == T - 1 and lagging(like, n, LAG + 2) and (n - LAG - 2) % 4 == 3:
                    context(r if n >= LAG + 2 else r - 1, (n - LAG - 2) % H // 4)

            SPARSE_STEPS = 2 + 2 * TOP_PIECES + 1 + 3

            def sparse_steps(b, h, k):
                return Steps(dve, f"sparse_steps{h}", b, SPARSE_STEPS, k)

            def top(b, h, piece_):
                n, replace = divmod(piece_, 2)
                whole, rest = n < KEEP // 8, KEEP % 8
                steps = sparse_steps(b, h, 2 + 2 * piece_)
                from_ = W if n else E
                tiles = (2 * h, 2 * h + 1)
                if piece_ == 0:
                    dve.wait_ge(sem("sp_exp"), T * b + 2 * (h + 1))
                steps.wait()
                if not whole and replace:
                    steps.did(dve.memset(top8[:, tiles[0]:tiles[1] + 1, rest:8], -1.0))
                    steps.wait()
                for i in tiles:
                    if replace:
                        steps.did(dve.match_replace(W[:, i, :], top8[:, i, :], from_[:, i, :], -1.0))
                    else:
                        steps.did(dve.max(top8[:, i, :], from_[:, i, :]))

            def stacks_at_rest():
                dve.memset(qst[:, :, :], 0.0).then_inc(sem("stack_init"), 1)
                dve.memset(kst[:, :, :], 0.0).then_inc(sem("stack_init"), 1)
                dve.memset(vp[:, :, :, :], 0.0).then_inc(sem("stack_init"), 1)
                dve.memset(zrows[:, :], 0.0).then_inc(sem("stack_init"), 1)
                dve.wait_ge(sem("stack_init"), 4)
                dve.memset(kst[MROW:MROW + PARTS, :, :], 1.0).then_inc(sem("stack_init"), 1)
                dve.memset(vp[:, :, :, DH:DH + 1], 1.0).then_inc(sem("stack_init"), 1)

            def piece(name, k, r, b):
                if name == "stats":
                    stats_of(k, b)
                elif name == "apply":
                    apply(k, b)
                    if k in ("L1", "L2") and last_period(r):
                        after_norm(dve, k, b)
                    if isinstance(r, int) and r == -1:
                        stacks_at_rest()
                elif name == "project_out":
                    dve.wait_ge(sem(f"proj_{k}"), b + 1)
                    dve.tensor_tensor(proj[:, :, :], misc_t, bc(f"bo_{k}"), ALU.add).then_inc(sem(f"proj_read_{k}"), 1)
                    dve.wait_ge(sem(f"proj_read_{k}"), b + 1)
                    if k == "A":
                        dve.tensor_tensor(batch(b), batch(b), proj[:, :, :], ALU.add).then_inc(sem("x_attn"), 1)
                    else:
                        dve.wait_ge(sem("sp_out_read"), T * (b + 1))
                        dve.scalar_tensor_tensor(x1[:, :, :], proj[:, :, :], sig[:, 2:3], batch(b, base),
                                                 ALU.mult, ALU.add).then_inc(sem("x1_ready"), 1)
                elif name == "rank":
                    dve.wait_ge(sem(f"gate_exp_{k}"), b + 1)
                    steps = Steps(dve, f"route_steps_{k}", b, T + 2)
                    for i in range(T):
                        steps.did(dve.scalar_tensor_tensor(junk[:, i, :], srow[:, :], scol[:, i:i + 1],
                                                           earlier[:, i, :], ALU.subtract, ALU.is_gt,
                                                           accum_out=rank[:, i:i + 1]))
                    steps.did(dve.tensor_scalar(gate[:, 1, :], gate[:, 0, :], 1.0, None, ALU.add))
                    steps.wait()
                    steps.did(dve.reciprocal(gate[:, 2, :], gate[:, 1, :]))
                    steps.wait()
                    steps.end()
                    dve.scalar_tensor_tensor(gate[:, 3, :], rank[:, :], float(ROUTED), gate[:, 2, :],
                                             ALU.is_lt, ALU.mult).then_inc(sem(f"gate_{k}"), 1)
                elif name == f"ffn_out{T - 1}" and k != "L1":
                    dve.wait_ge(sem(f"ffn_{k}"), b + 1)
                    dve.tensor_tensor(upd[:, :, :], misc_t, bc("b2"), ALU.add).then_inc(sem(f"ffn_read_{k}"), 1)
                elif name == f"ffn_out{T - 1}":
                    dve.wait_ge(sem("ffn_L1"), b + 1)
                    dve.tensor_tensor(y1[:, :, :], misc_t, bc("ff2b"), ALU.add).then_inc(sem("ffn_read_L1"), 1)
                    dve.wait_ge(sem("ffn_read_L1"), b + 1)
                    dve.tensor_tensor(y1[:, :, :], y1[:, :, :], x1n[:, :, :], ALU.add).then_inc(sem("y1_ready"), 1)
                elif name == "update":
                    dve.wait_ge(sem(f"gate_{k}"), b + 1)
                    dve.wait_ge(sem(f"ffn_read_{k}"), b + 1)
                    steps = Steps(dve, f"update_steps_{k}", b, T)
                    for i in range(T):
                        steps.did(dve.scalar_tensor_tensor(upd[:, i, :], upd[:, i, :], gate[:, 3, i:i + 1],
                                                           xn[k][:, i, :], ALU.mult, ALU.add))
                    steps.wait()
                    steps.end()
                    dve.tensor_tensor(batch(b), batch(b), upd[:, :, :], ALU.add).then_inc(sem(X_DONE[k]), 1)
                elif name == "sparse_v":
                    dve.wait_ge(sem("sp_v"), b + 1)
                    dve.tensor_tensor(vsp[:, :, :], misc_t, bc("bvp"), ALU.add).then_inc(sem("sp_v_in"), 1)
                elif name == "sparse_score":
                    steps = sparse_steps(b, k // 2, k % 2)
                    dve.wait_ge(sem("sp_score"), T * b + k + 1)
                    steps.did(dve.tensor_reduce(smax[:, 0, k:k + 1], misc[:, :], AX.X, ALU.max))
                    steps.wait()
                    dve.tensor_scalar(smax[:, 1, k:k + 1], smax[:, 0, k:k + 1], -R ** -0.5, None, ALU.mult
                                      ).then_inc(sem("sp_bias"), 1)
                elif name == "top":
                    top(b, *k)
                elif name == "sparse_keep":
                    steps = sparse_steps(b, k, SPARSE_STEPS - 3)
                    steps.wait()
                    for i in (2 * k, 2 * k + 1):
                        dve.scalar_tensor_tensor(W[:, i, :], W[:, i, :], 0.0, E[:, i, :], ALU.is_lt, ALU.mult,
                                                 accum_out=ssel[:, i:i + 1]).then_inc(sem("sp_kept"), 1)
                    dve.wait_ge(sem("sp_kept"), T * b + 2 * (k + 1))
                    half_ = slice(2 * k, 2 * k + 2)
                    steps.did(dve.scalar_tensor_tensor(rsp[:, 0, half_], sall[:, half_], 1e-9, ssel[:, half_],
                                                       ALU.mult, ALU.add))
                    steps.wait()
                    steps.did(dve.reciprocal(rsp[:, 1, half_], rsp[:, 0, half_]))
                    steps.wait()
                    steps.did(dve.tensor_scalar(rsp[:, 0, half_], rsp[:, 1, half_], sig[:, 3:4], None, ALU.mult))
                    steps.end()
                elif name in ("sparse_out1", "sparse_out3"):
                    h = int(name == "sparse_out3")
                    dve.wait_ge(sem(f"sparse_steps{h}"), SPARSE_STEPS * (b + 1))
                    dve.wait_ge(sem("sp_out"), 2 * b + h + 1)
                    for i in (2 * h, 2 * h + 1):
                        dve.scalar_tensor_tensor(base[:, b * T + i, :], misc_t[:, i, :], rsp[:, 0, i:i + 1],
                                                 base[:, b * T + i, :], ALU.mult, ALU.add
                                                 ).then_inc(sem("sp_out_read"), 1)

            def rest_of_setup():
                dve.wait_ge(sem("w_in"), DMA * W_DMAS)
                dve.wait_ge(sem("earlier_ready"), 1)
                dve.tensor_copy(wr[:, :], wr_col[:, :].broadcast_to([P, P])).then_inc(sem("wr_ready"), 1)
                dve.wait_ge(sem("lam_exp"), 1)
                dve.tensor_scalar(sig[:, 1:2], sig[:, 0:1], 1.0, None, ALU.add).then_inc(sem("sig_steps"), 1)
                dve.wait_ge(sem("sig_steps"), 1)
                dve.reciprocal(sig[:, 2:3], sig[:, 1:2]).then_inc(sem("sig_steps"), 1)
                dve.wait_ge(sem("sig_steps"), 2)
                dve.tensor_scalar(sig[:, 3:4], sig[:, 2:3], -1.0, 1.0, ALU.mult, ALU.add).then_inc(sem("sig_steps"), 1)
                dve.wait_ge(sem("sig_steps"), 3)

            dve.wait_ge(sem("w_first"), DMA * W_FIRST)
            run(dve, core, piece)


def kernel(**inputs):
    import concourse.bacc as bacc
    from concourse.bass_utils import run_bass_kernel_spmd

    a = {k: np.asarray(v) for k, v in inputs.items()}
    m = np.arange(D)

    def circulant(name):
        return a[name][(m[None, :] - m[:, None]) % D]

    A, L = "L0_attn_a_", "L0_attn_b_"
    arrays = {
        "x": a[A + "x"].reshape(B * SEQ, D),
        "w_A": np.stack([circulant(f"{A}w{n}_c") for n in "qkv"], 1),
        "wo_A": circulant(A + "wo_c"),
        "b_A": np.concatenate([a[f"{A}w{n}_b"] for n in "qkv"]),
        "bo_A": a[A + "wo_b"],
        "w_B": a[L + "in_proj_w"].T.reshape(D, 3, D),
        "wo_B": a[L + "out_proj_w"].T,
        "b_B": a[L + "in_proj_b"],
        "bo_B": a[L + "out_proj_b"],
        "QpT": a[L + "Qp_w"].T, "Qpb": a[L + "Qp_b"],
        "KpT": a[L + "Kp_w"].T, "Kpb": a[L + "Kp_b"],
        "VpT": a[L + "Vp_w"].T, "Vpb": a[L + "Vp_b"],
        "lam": a[L + "lam"].reshape(1),
        "ff1T": a[L + "ff1_w"].T, "ff1b": a[L + "ff1_b"].reshape(FT, P).T,
        "ff2T": a[L + "ff2_w"].T, "ff2b": a[L + "ff2_b"],
        "ln1g": a[L + "ln1_g"], "ln1b": a[L + "ln1_b"], "ln2g": a[L + "ln2_g"], "ln2b": a[L + "ln2_b"],
        "wr": a["L0_ffn_w_router"], "W1": a["L0_ffn_W1"], "b1": a["L0_ffn_b1"].reshape(FT, P).T,
        "W2": a["L0_ffn_W2"], "b2": a["L0_ffn_b2"],
    }
    arrays = {k: np.ascontiguousarray(v) for k, v in arrays.items()}
    nc = bacc.Bacc("TRN2", target_bir_lowering=False, num_devices=1)
    t = {k: nc.dram_tensor(f"in_{k}", v.shape, F32, kind="ExternalInput").ap() for k, v in arrays.items()}
    t["out"] = nc.dram_tensor("out", (B * SEQ, D), F32, kind="ExternalOutput").ap()
    build(nc, t)
    r = run_bass_kernel_spmd(nc, [{f"in_{k}": v for k, v in arrays.items()}], core_ids=[0])
    return r.results[0]["out"].reshape(B, SEQ, D)
```
